# Optimizing a Trainium2 kernel written in Bass

```python
import numpy as np
import jax
import jax.numpy as jnp

def _softmax(x, axis=-1):
    return jax.nn.softmax(x, axis=axis)

def _gelu(x):
    return jax.nn.gelu(x, approximate=True)

def _silu(x):
    return jax.nn.silu(x)

def _sigmoid(x):
    return jax.nn.sigmoid(x)

def _layernorm(x, axis=-1, eps=1e-05):
    m = jnp.mean(x, axis=axis, keepdims=True)
    v = jnp.var(x, axis=axis, keepdims=True)
    return (x - m) / jnp.sqrt(v + eps)

def _scatter_add(tgt, idx, src, axis=0):
    return tgt.at[idx].add(src)

def _segment_sum(src, seg, n):
    return jax.ops.segment_sum(src, seg, n)
kernel_name = 'mk_prb_d1_jaxref_r8_5c60a5'

def setup_inputs(seed: int=0):
    np.random.seed(seed)
    _w = jnp.asarray

    def _L0_attn_setup():
        import jax, jax.numpy as jnp
        import numpy as np
        import math
        DIM = 128
        NUM_HEADS = 16
        HEAD_DIM = DIM // NUM_HEADS
        BATCH = 4
        SEQ = 512

        def _feature_map(x, R):
            x = x / math.sqrt(HEAD_DIM)
            proj = jnp.einsum('bhnd,dm->bhnm', x, R)
            sq_norm = jnp.sum(x * x, axis=-1, keepdims=True)
            return jnp.exp(proj - 0.5 * sq_norm)
        key = jax.random.key(seed)
        ks = jax.random.split(key, 10)
        s = 1.0 / math.sqrt(DIM)
        return {'x': jax.random.normal(ks[0], (BATCH, SEQ, DIM), dtype=jnp.float32), 'Wq': jax.random.normal(ks[1], (DIM, DIM), dtype=jnp.float32) * s, 'bq': jax.random.normal(ks[2], (DIM,), dtype=jnp.float32) * 0.01, 'Wk': jax.random.normal(ks[3], (DIM, DIM), dtype=jnp.float32) * s, 'bk': jax.random.normal(ks[4], (DIM,), dtype=jnp.float32) * 0.01, 'Wv': jax.random.normal(ks[5], (DIM, DIM), dtype=jnp.float32) * s, 'bv': jax.random.normal(ks[6], (DIM,), dtype=jnp.float32) * 0.01, 'Wo': jax.random.normal(ks[7], (DIM, DIM), dtype=jnp.float32) * s, 'bo': jax.random.normal(ks[8], (DIM,), dtype=jnp.float32) * 0.01, 'R': jax.random.normal(ks[9], (HEAD_DIM, HEAD_DIM), dtype=jnp.float32) * 0.4}
    _L0_attn_in = _L0_attn_setup()

    def _L0_ffn_setup():
        import jax, jax.numpy as jnp
        import numpy as np
        B, N, C, F, E, K = (2, 256, 128, 512, 8, 2)
        key = jax.random.key(seed)
        k = jax.random.split(key, 6)
        xavier1 = float(np.sqrt(6.0 / (C + F)))
        xavier2 = float(np.sqrt(6.0 / (F + C)))
        return {'x': jax.random.normal(k[0], (B, N, C), dtype=jnp.float32), 'router_w': jax.random.normal(k[1], (E, C), dtype=jnp.float32) * 0.01, 'w1': jax.random.uniform(k[2], (E, F, C), dtype=jnp.float32, minval=-xavier1, maxval=xavier1), 'b1': jnp.zeros((E, F), dtype=jnp.float32), 'w2': jax.random.uniform(k[3], (E, C, F), dtype=jnp.float32, minval=-xavier2, maxval=xavier2), 'b2': jnp.zeros((E, C), dtype=jnp.float32)}
    _L0_ffn_in = _L0_ffn_setup()
    _d = {'L0_attn_x': _L0_attn_in['x'], 'L0_attn_Wq': _L0_attn_in['Wq'], 'L0_attn_bq': _L0_attn_in['bq'], 'L0_attn_Wk': _L0_attn_in['Wk'], 'L0_attn_bk': _L0_attn_in['bk'], 'L0_attn_Wv': _L0_attn_in['Wv'], 'L0_attn_bv': _L0_attn_in['bv'], 'L0_attn_Wo': _L0_attn_in['Wo'], 'L0_attn_bo': _L0_attn_in['bo'], 'L0_attn_R': _L0_attn_in['R'], 'L0_ffn_router_w': _L0_ffn_in['router_w'], 'L0_ffn_w1': _L0_ffn_in['w1'], 'L0_ffn_b1': _L0_ffn_in['b1'], 'L0_ffn_w2': _L0_ffn_in['w2'], 'L0_ffn_b2': _L0_ffn_in['b2']}
    _x0 = _d['L0_attn_x']
    _d['L0_attn_x'] = jax.random.normal(jax.random.fold_in(jax.random.key(seed), 1), (16, 256, 128), dtype=_x0.dtype)
    del _x0
    return _d

def reference(L0_attn_x, L0_attn_Wq, L0_attn_bq, L0_attn_Wk, L0_attn_bk, L0_attn_Wv, L0_attn_bv, L0_attn_Wo, L0_attn_bo, L0_attn_R, L0_ffn_router_w, L0_ffn_w1, L0_ffn_b1, L0_ffn_w2, L0_ffn_b2):

    def _L0_attn_ref(x, Wq, bq, Wk, bk, Wv, bv, Wo, bo, R):
        import jax, jax.numpy as jnp
        import numpy as np
        import math
        DIM = 128
        NUM_HEADS = 16
        HEAD_DIM = DIM // NUM_HEADS
        BATCH = 4
        SEQ = 512

        def _feature_map(x, R):
            x = x / math.sqrt(HEAD_DIM)
            proj = jnp.einsum('bhnd,dm->bhnm', x, R)
            sq_norm = jnp.sum(x * x, axis=-1, keepdims=True)
            return jnp.exp(proj - 0.5 * sq_norm)
        b, n, _ = x.shape
        h, d = (NUM_HEADS, HEAD_DIM)

        def split_heads(t):
            return t.reshape(b, n, h, d).transpose(0, 2, 1, 3)
        q = split_heads(x @ Wq.T + bq)
        k = split_heads(x @ Wk.T + bk)
        v = split_heads(x @ Wv.T + bv)
        q_prime = _feature_map(q, R)
        k_prime = _feature_map(k, R)
        kv = jnp.einsum('bhnd,bhne->bhde', k_prime, v)
        z = 1.0 / (jnp.sum(q_prime, axis=-1) + 1e-08)
        out = jnp.einsum('bhnd,bhde,bhn->bhne', q_prime, kv, z)
        out = out.transpose(0, 2, 1, 3).reshape(b, n, DIM)
        return out @ Wo.T + bo

    def _L0_ffn_ref(x, router_w, w1, b1, w2, b2):
        import jax, jax.numpy as jnp
        import numpy as np
        B, N, C, F, E, K = (2, 256, 128, 512, 8, 2)
        Bb, Nn, Cc = x.shape
        x_flat = x.reshape(-1, Cc)
        logits = jnp.einsum('tc,ec->te', x_flat, router_w)
        probs = jax.nn.softmax(logits, axis=-1)
        top_w, top_idx = jax.lax.top_k(probs, K)
        top_w = top_w / (jnp.sum(top_w, axis=-1, keepdims=True) + 1e-09)
        h = jnp.einsum('tc,efc->tef', x_flat, w1) + b1[None]
        h = jax.nn.relu(h)
        y = jnp.einsum('tef,ecf->tec', h, w2) + b2[None]
        sel = jnp.take_along_axis(y, top_idx[:, :, None], axis=1)
        out = jnp.einsum('tkc,tk->tc', sel, top_w)
        return out.reshape(Bb, Nn, Cc)
    x = L0_attn_x
    xn = _layernorm(x, axis=-1)
    x = x + _L0_attn_ref(xn, L0_attn_Wq, L0_attn_bq, L0_attn_Wk, L0_attn_bk, L0_attn_Wv, L0_attn_bv, L0_attn_Wo, L0_attn_bo, L0_attn_R) + _L0_ffn_ref(xn, L0_ffn_router_w, L0_ffn_w1, L0_ffn_b1, L0_ffn_w2, L0_ffn_b2)
    return x

_drawn_inputs = setup_inputs


def setup_inputs(seed=0):
    import zlib

    import numpy as np

    out = dict(_drawn_inputs(seed))
    spreads = {'L0_ffn_b1': (0.0, 0.8), 'L0_ffn_b2': (0.0, 0.8)}
    factors = {'L0_attn_bq': 31.113, 'L0_attn_bk': 8.0, 'L0_attn_bo': 58.347}
    for name, (base, spread) in spreads.items():
        noise = np.random.default_rng([zlib.crc32(name.encode()), seed]).standard_normal(out[name].shape)
        drawn = base * np.exp(spread * noise) if base else spread * noise
        out[name] = jnp.asarray(drawn.astype(out[name].dtype))
    for name, factor in factors.items():
        out[name] = (out[name] * factor).astype(out[name].dtype)
    return out
```

```python
from contextlib import ExitStack

import concourse.bass as bass
from concourse import mybir

F32 = mybir.dt.float32
F16 = mybir.dt.float16
BF16 = mybir.dt.bfloat16
I32 = mybir.dt.int32
ALU = mybir.AluOpType
ACT = mybir.ActivationFunctionType
AX = mybir.AxisListType
ds = bass.ds

P = 128
C = 128
HEADS, HD = 16, 8
E, F = 8, 512
FC = F // P
WS = 16.0
RS = 1024.0
Q, K, V, PQ, PK = range(5)


def build(nc, x, wq, wk, wqT, wkT, wvT, woT, bq, bk, bv, bo, R, rwT, w1T, b1, w2T, b2, out):
    T = x.shape[0] * x.shape[1]
    NJ = T // P
    GT = 4
    GN = GT * P
    NG = NJ // GT
    NT = 2 * T // P + E
    PAIRS = 2 * T
    assert NT % 4 == 0 and x.shape[1] == 2 * P

    x_rows = x.rearrange("b n c -> (b n) c")
    out_rows = out.rearrange("b n c -> (b n) c")
    xn_dram = nc.dram_tensor("xn_dram", [T, 2 * C], F16).ap()
    y_dram = nc.dram_tensor("y_dram", [PAIRS + 4 * P, C], F32).ap()

    with ExitStack() as ctx:
        def sb(name, shape, dt=F32):
            return ctx.enter_context(nc.sbuf_tensor(name, shape, dt))

        def sem(name):
            return ctx.enter_context(nc.semaphore(name))

        bank = [ctx.enter_context(nc.psum_tensor(f"bank{i}", [P, 512], F32)) for i in range(8)]

        xin = sb("xin", [P, NJ, C])
        xs = sb("xs", [P, NJ, 2, C], F16)
        xT = sb("xT", [P, 2, T], F16)
        xg = sb("xg", [P, NT, 2 * C], F16)
        w1h = sb("w1h", [P, E * F], F16)
        w1l = sb("w1l", [P, E * F], F16)
        w2h = sb("w2h", [P, E * FC * C], F16)
        w2l = sb("w2l", [P, E * FC * C], F16)
        wraw = sb("wraw", [P, E * F])
        wraw2 = sb("wraw2", [P, E * F])
        wnat = sb("wnat", [P, 2, C])
        w3 = sb("w3", [P, 3, C])
        wo_sb = sb("wo_sb", [P, C])
        WH = sb("WH", [P, 5, C], F16)
        WL = sb("WL", [P, 5, C], F16)
        r_rep = sb("r_rep", [P, HD])
        rblk = sb("rblk", [P, C])
        rw_raw = sb("rw_raw", [P, E])
        rw = sb("rw", [P, 2, E], F16)
        bqk = sb("bqk", [P, 2])
        bk_wide = sb("bk_wide", [P, C])
        bpq = sb("bpq", [P, 1])
        bv_bc = sb("bv_bc", [P, C])
        bo_bc = sb("bo_bc", [P, C])
        kb_rows = sb("kb_rows", [P, C], F16)
        kb_hi = sb("kb_hi", [P, C], F16)
        b1_raw = sb("b1_raw", [36, E, P])
        b1_hi = sb("b1_hi", [36, E, P], F16)
        b1_rows = sb("b1_rows", [P, E * P], F16)
        b2_raw = sb("b2_raw", [33, E, C])
        b2_hi = sb("b2_hi", [33, E, C], F16)
        b2_rows = sb("b2_rows", [P, E * C], F16)
        id16 = sb("id16", [P, P], F16)
        id32 = sb("id32", [P, P])
        ones16 = sb("ones16", [P, P], F16)
        onesb = sb("onesb", [P, P], BF16)
        before = sb("before", [P, P], BF16)
        blk = sb("blk", [P, HEADS, HD])
        negblk = sb("negblk", [P, C])
        headof = sb("headof", [P, HEADS])
        chunk_of = sb("chunk_of", [P, FC, P], F16)
        rank8 = sb("rank8", [P, E])
        iota_e = sb("iota_e", [P, P], BF16)
        iota_t = sb("iota_t", [P, NT])
        jcol = sb("jcol", [P, 2 * NJ])
        p1col = sb("p1col", [P, 1])
        waste = sb("waste", [P, NT])
        ones_row = sb("ones_row", [P, E * NJ])
        st6 = sb("st6", [P, 2, GT, 6])
        mv = sb("mv", [P, 2, GT, 2])
        veps = sb("veps", [P, 2, GT])
        sd = sb("sd", [P, 2, GT])
        rs0 = sb("rs0", [P, GT])
        rs1 = sb("rs1", [P, GT])
        rs2 = sb("rs2", [P, GT])
        rstd = sb("rstd", [P, GT])
        xn = sb("xn", [P, 2, GT, C])
        lg = sb("lg", [P, NJ, E])
        m1 = sb("m1", [P, NJ])
        m2 = sb("m2", [P, NJ])
        eq = sb("eq", [P, NJ, E])
        sc = sb("sc", [P, NJ, E])
        mx = sb("mx", [P, NJ])
        pick1 = sb("pick1", [P, NJ, E])
        pick2 = sb("pick2", [P, NJ, E])
        lg2 = sb("lg2", [P, NJ, E])
        dlt = sb("dlt", [P, NJ, E])
        d2 = sb("d2", [P, NJ])
        ex = sb("ex", [P, NJ, E])
        ex2 = sb("ex2", [P, NJ])
        ssum = sb("ssum", [P, NJ])
        pr1 = sb("pr1", [P, NJ])
        pr2 = sb("pr2", [P, NJ])
        den = sb("den", [P, NJ])
        rden = sb("rden", [P, NJ])
        gate1 = sb("gate1", [P, NJ])
        gate2 = sb("gate2", [P, NJ])
        took = sb("took", [P, E, NJ], BF16)
        tot = sb("tot", [P, E, NJ])
        run = sb("run", [P, E, NJ])
        exc = sb("exc", [P, E, NJ])
        cnt = sb("cnt", [P, E])
        cnt_i = sb("cnt_i", [P, E], I32)
        nt_i = sb("nt_i", [P, E], I32)
        nt_f = sb("nt_f", [P, E])
        end_t = sb("end_t", [P, E])
        base = sb("base", [P, E])
        offs = sb("offs", [P, E])
        pos = sb("pos", [P, E, NJ])
        pos2 = sb("pos2", [P, E, NJ])
        ppick = sb("ppick", [P, NJ, E])
        slot = sb("slot", [P, 2 * NJ])
        slot_i = sb("slot_i", [P, 2 * NJ], I32)
        lo_i = sb("lo_i", [P, 2 * NJ], I32)
        hi_i = sb("hi_i", [P, 2 * NJ], I32)
        lo_f = sb("lo_f", [P, 2 * NJ])
        hi_f = sb("hi_f", [P, 2 * NJ])
        cmp_t = sb("cmp_t", [P, NT, E])
        et_f = sb("et_f", [P, NT])
        et_i = sb("et_i", [P, NT], I32)
        oh_lo = sb("oh_lo", [P, 4, P], BF16)
        oh_hi = sb("oh_hi", [P, 4, 2 * NT], BF16)
        ip = sb("ip", [P, NT])
        idf = sb("idf", [P, NT])
        inv = sb("inv", [P, NT])
        gidf = sb("gidf", [P, NT])
        gid_i = sb("gid_i", [P, NT], I32)
        gid = sb("gid", [P, NT], I32)
        sid_f = sb("sid_f", [P, NT])
        sid = sb("sid", [P, NT], I32)
        free = xs[:, :, :, :].rearrange("p j s c -> p (j s c)").bitcast(F32)
        q2, k2, qf, kf2, vv2, oo2, oT, kvm2 = (free[:, i * GN:(i + 1) * GN] for i in range(8))
        kf, vv, oo = (a.rearrange("p (j c) -> p j c", j=GT) for a in (kf2, vv2, oo2))
        kvm = kvm2[:, 0:2 * C].rearrange("p (b c) -> p b c", b=2)
        zz = sb("zz", [P, 2, 2, HEADS])
        zr = sb("zr", [P, 2, 2, HEADS])
        free2 = xT[:, :, :].rearrange("p s n -> p (s n)")
        xgT = free2[:, 0:4 * P].rearrange("p (b s n) -> p b s n", b=2, s=2)
        hh = free2[:, 1024:1024 + 2 * F].rearrange("p (b f) -> p b f", b=2)
        hl = free2[:, 2048:2048 + 2 * F].rearrange("p (b f) -> p b f", b=2)
        yb = free2[:, 3072:3072 + 8 * C].bitcast(F32).rearrange("p (b c) -> p b c", b=4)

        names = """consts wsmall_in w1_in w2_in biases_in
            x_landed stats sd_ready xn_ready hi_ready lo_ready xb_ready xT_tr xT_ready xs_stored
            setup_dve setup_pe setup_act small_split rw_ready w_split wsplit_hi
            logits counts took_ready exp_in exp_out perm_in onehot perm_used perm ids_ready dve
            q_proj k_proj q_expo k_expo v_proj kv_sum nums o_trans wo_out
            q_sq k_sq q_feat k_feat oT_ready v_ready kv_ready o_ready acc_ready
            gathered slots_tr slots_ready h_ready hh_ready hl_ready y_ready y_out y_free
            scattered summed stored""".split()
        S = {n: sem(n) for n in names}
        x_in = [sem(f"x_in{i}") for i in range(4)]
        gather_in = [sem(f"gather_in{i}") for i in range(4)]
        scatter_in = [sem(f"scatter_in{i}") for i in range(4)]
        y_in = [sem(f"y_in{i}") for i in range(4)]

        block = ctx.enter_context(nc.Block())
        NW, NB = 8, 8

        @block.sync
        def _(sp):
            XQ = NJ // 4
            for i in range(4):
                sp.dma_start(xin[:, i * XQ:(i + 1) * XQ, :],
                             x_rows[i * XQ * P:(i + 1) * XQ * P].rearrange("(j p) c -> p j c", p=P)).then_inc(x_in[i], 16)
            for i in range(4):
                sp.wait_ge(x_in[i], 16)
                sp.sem_inc(S["x_landed"], NG // 4)
            with sp.Fori(0, NG) as g:
                sp.wait_ge(S["hi_ready"], g + 1)
                sp.wait_ge(S["lo_ready"], g + 1)
                sp.dma_start(xn_dram[ds(g * GN, GN), :].rearrange("(j p) c -> p j c", p=P),
                             xs[:, ds(g * GT, GT), :, :].rearrange("p j s c -> p j (s c)")).then_inc(S["xs_stored"], 16)
            for i in range(4):
                sp.wait_ge(scatter_in[i], 16 * (NT // 4))
            sp.wait_ge(S["w_split"], 2)
            for i in range(4):
                for k, dst in ((0, wraw), (1, wraw2)):
                    rows = y_dram[k * T + i * XQ * P:k * T + (i + 1) * XQ * P]
                    sp.dma_start(dst[:, i * XQ * C:(i + 1) * XQ * C].rearrange("p (j c) -> p j c", c=C),
                                 rows.rearrange("(j p) c -> p j c", p=P)).then_inc(y_in[i], 16)
            for i in range(4):
                sp.wait_ge(S["summed"], (i + 1) * XQ)
                sp.dma_start(out_rows[i * XQ * P:(i + 1) * XQ * P].rearrange("(j p) c -> p j c", p=P),
                             xin[:, i * XQ:(i + 1) * XQ, :]).then_inc(S["stored"], 16)
            sp.wait_ge(S["stored"], 64)

        @block.gpsimd
        def _(po):
            n = [0]

            def made(ins):
                ins.then_inc(S["consts"], 1)
                n[0] += 1
                po.wait_ge(S["consts"], n[0])

            def select(t, op, basev, pattern, cm, fill):
                made(po.affine_select(out=t, in_=t, compare_op=op, fill=fill, base=basev, pattern=pattern,
                                      channel_multiplier=cm))

            made(po.memset(id16[:, :], 0.0))
            select(id16[:, :], ALU.not_equal, 0, [[-1, P]], 1, 1.0)
            made(po.memset(id32[:, :], 0.0))
            select(id32[:, :], ALU.not_equal, 0, [[-1, P]], 1, 1.0)
            made(po.memset(blk[:, :, :], 1.0))
            select(blk[:, :, :], ALU.is_ge, 0, [[-HD, HEADS], [0, HD]], 1, 0.0)
            select(blk[:, :, :], ALU.is_ge, HD - 1, [[HD, HEADS], [0, HD]], -1, 0.0)
            made(po.memset(headof[:, :], 1.0))
            select(headof[:, :], ALU.is_ge, 0, [[-HD, HEADS]], 1, 0.0)
            select(headof[:, :], ALU.is_ge, HD - 1, [[HD, HEADS]], -1, 0.0)
            made(po.memset(before[:, :], 1.0))
            select(before[:, :], ALU.is_ge, -1, [[1, P]], -1, 0.0)
            made(po.memset(chunk_of[:, :, :], 0.0))
            select(chunk_of[:, :, :], ALU.not_equal, 0, [[-1, FC], [0, P]], 1, 1.0)
            select(chunk_of[:, :, :], ALU.not_equal, -32, [[-1, FC], [0, P]], 1, 1.0)
            made(po.memset(ones16[:, :], 1.0))
            made(po.memset(onesb[:, :], 1.0))
            made(po.memset(ones_row[:, :], 1.0))
            made(po.memset(b1_rows[:, :], 0.0))
            made(po.memset(b2_rows[:, :], 0.0))
            made(po.memset(kb_rows[:, :], 0.0))
            made(po.iota(rank8[:, :], [[-1, E]], base=E, channel_multiplier=0, allow_small_or_imprecise_dtypes=True))
            made(po.iota(iota_e[:, :], [[1, P]], base=0, channel_multiplier=0, allow_small_or_imprecise_dtypes=True))
            made(po.iota(iota_t[:, :], [[1, NT]], base=0, channel_multiplier=0, allow_small_or_imprecise_dtypes=True))
            made(po.iota(jcol[:, :], [[1, 2 * NJ]], base=0, channel_multiplier=0, allow_small_or_imprecise_dtypes=True))
            made(po.iota(p1col[:, :], [[0, 1]], base=1, channel_multiplier=1, allow_small_or_imprecise_dtypes=True))
            made(po.iota(waste[:, :], [[0, NT // 4], [P, 4]], base=PAIRS + 1, channel_multiplier=1, allow_small_or_imprecise_dtypes=True))
            assert n[0] == NCONST
            po.wait_ge(S["biases_in"], 16 * NB)
            with po.Fori(0, NG) as g:
                po.wait_ge(S["hi_ready"], g + 1)
                po.tensor_tensor(xs[:, ds(g * GT, GT), 1, :], xn[:, ds(g % 2, 1), :, :].rearrange("p a j c -> p (a j) c"),
                                 xs[:, ds(g * GT, GT), 0, :], ALU.subtract).then_inc(S["lo_ready"], 1)
                po.tensor_tensor(xin[:, ds(g * GT, GT), :], xin[:, ds(g * GT, GT), :],
                                 bo_bc[:, :].unsqueeze(1).to_broadcast([P, GT, C]), ALU.add).then_inc(S["xb_ready"], 1)
            po.wait_ge(S["ids_ready"], 3)
            po.wait_ge(S["xs_stored"], 16 * NG)

            for t in range(NT):
                if t >= 4:
                    po.wait_ge(gather_in[t % 4], t // 4 * 16)
                    po.sem_inc(S["gathered"], 1)
                po.indirect_dma_start(out=xg[:, t, :], out_offset=None, in_=xn_dram,
                                      in_offset=bass.IndirectOffsetOnAxis(ap=gid[:, t:t + 1], axis=0)).then_inc(gather_in[t % 4], 16)
            for t in range(4):
                po.wait_ge(gather_in[t], NT // 4 * 16)
                po.sem_inc(S["gathered"], 1)
            for t in range(NT):
                if t >= 4:
                    po.wait_ge(scatter_in[t % 4], t // 4 * 16)
                    po.sem_inc(S["y_free"], 1)
                po.wait_ge(S["y_out"], t + 1)
                po.indirect_dma_start(out=y_dram, out_offset=bass.IndirectOffsetOnAxis(ap=sid[:, t:t + 1], axis=0),
                                      in_=yb[:, t % 4, :], in_offset=None).then_inc(scatter_in[t % 4], 16)

        @block.scalar
        def _(ac):
            for dst, src in ((wnat[:, 0, :], wq), (wnat[:, 1, :], wk), (w3[:, 0, :], wqT), (w3[:, 1, :], wkT),
                             (w3[:, 2, :], wvT), (wo_sb[:, :], woT), (rw_raw[:, :], rwT),
                             (r_rep[:, :], R)):
                ac.dma_start(dst, src).then_inc(S["wsmall_in"], 16)
            for dst, src in ((bqk[:, 0:1], bq), (bqk[:, 1:2], bk), (bv_bc[:, :], bv.partition_broadcast(P)),
                             (bo_bc[:, :], bo.partition_broadcast(P)), (b1_raw[0:4, :, :], b1), (b1_raw[32:36, :, :], b1),
                             (b2_raw[0:1, :, :], b2), (b2_raw[32:33, :, :], b2)):
                ac.dma_start(dst, src).then_inc(S["biases_in"], 16)
            ac.dma_start(wraw[:, :], w1T).then_inc(S["w1_in"], 16)
            ac.dma_start(wraw2[:, :], w2T).then_inc(S["w2_in"], 16)

            def deviation(g, b):
                ac.wait_ge(S["stats"], g + 1)
                ac.activation(sd[:, b, :], veps[:, b, :], ACT.Sqrt).then_inc(S["sd_ready"], 1)

            def high(g, b):
                ac.wait_ge(S["xn_ready"], g + 1)
                ac.activation(xs[:, ds(g * GT, GT), 0, :], xn[:, b, :, :], ACT.Copy).then_inc(S["hi_ready"], 1)

            def transposed(g, b):
                ac.wait_ge(S["xT_tr"], g + 1)
                ac.activation(xT[:, :, ds(g * GN, GN)],
                              bank[b][:, :].bitcast(F16).rearrange("p (s n) -> p s n", s=2), ACT.Copy).then_inc(S["xT_ready"], 1)

            deviation(0, 0)
            deviation(1, 1)
            high(0, 0)
            with ac.Fori(0, NG // 2 - 1) as r:
                deviation(r * 2 + 2, 0)
                high(r * 2 + 1, 1)
                transposed(r * 2, 0)
                deviation(r * 2 + 3, 1)
                high(r * 2 + 2, 0)
                transposed(r * 2 + 1, 1)
            high(NG - 1, 1)
            transposed(NG - 2, 0)
            transposed(NG - 1, 1)
            ac.wait_ge(S["exp_in"], 2)
            ac.activation(ex[:, :, :], dlt[:, :, :], ACT.Exp, scale=1.0 / RS).then_inc(S["exp_out"], 1)
            ac.activation(ex2[:, :], d2[:, :], ACT.Exp, scale=1.0 / RS).then_inc(S["exp_out"], 1)
            ac.wait_ge(S["w1_in"], 16)
            ac.activation(w1h[:, :], wraw[:, :], ACT.Copy, scale=WS).then_inc(S["wsplit_hi"], 1)
            ac.wait_ge(S["w2_in"], 16)
            ac.activation(w2h[:, :], wraw2[:, :], ACT.Copy, scale=WS).then_inc(S["wsplit_hi"], 1)
            ac.wait_ge(S["setup_dve"], SETUP_BPQ)

            def square(ready, g, dst, b, done):
                ac.wait_ge(ready, g + 1)
                ac.activation(dst, bank[0][:, :], ACT.Square, scale=1.0 / WS, bias=bqk[:, b:b + 1]).then_inc(done, 1)

            def features(g):
                ac.wait_ge(S["q_expo"], g + 1)
                ac.activation(qf[:, :], bank[1][:, :], ACT.Exp, scale=1.0 / WS, bias=bpq[:, 0:1]).then_inc(S["q_feat"], 1)
                ac.wait_ge(S["k_expo"], g + 1)
                ac.activation(kf[:, :, :].rearrange("p j c -> p (j c)"), bank[2][:, :], ACT.Exp, scale=1.0 / WS).then_inc(S["k_feat"], 1)

            def attended(g):
                ac.wait_ge(S["o_trans"], g + 1)
                ac.activation(oT[:, :], bank[7][:, :], ACT.Copy).then_inc(S["oT_ready"], 1)

            def act_group(g, first=False, last=False):
                if not first:
                    attended(g - 1)
                features(g)
                if not last:
                    square(S["q_proj"], g + 1, q2[:, :], 0, S["q_sq"])
                    square(S["k_proj"], g + 1, k2[:, :], 1, S["k_sq"])

            square(S["q_proj"], 0, q2[:, :], 0, S["q_sq"])
            square(S["k_proj"], 0, k2[:, :], 1, S["k_sq"])
            act_group(0, first=True)
            with ac.Fori(1, NG - 1) as g:
                act_group(g)
            act_group(NG - 1, last=True)
            attended(NG - 1)

            def hidden(t, b):
                ac.wait_ge(S["h_ready"], t + 1)
                ac.activation(hh[:, b, :], bank[2 + b][:, :], ACT.Relu).then_inc(S["hh_ready"], 1)

            def output(t, u, wait_free=True):
                ac.wait_ge(S["y_ready"], t + 1)
                if wait_free:
                    ac.wait_ge(S["y_free"], t - 3)
                ac.activation(yb[:, u, :], bank[4 + u % 2][:, 0:C], ACT.Copy, scale=1.0 / (WS * WS)).then_inc(S["y_out"], 1)

            hidden(0, 0)
            for t in range(4):
                hidden(t + 1, (t + 1) % 2)
                output(t, t, wait_free=False)
            with ac.Fori(1, NT // 4 - 1) as r:
                for u in range(4):
                    hidden(r * 4 + u + 1, (u + 1) % 2)
                    output(r * 4 + u, u)
            for t in range(NT - 4, NT):
                if t + 1 < NT:
                    hidden(t + 1, (t + 1) % 2)
                output(t, t % 4)

        @block.vector
        def _(ve):
            n = [0]

            def step(ins):
                ins.then_inc(S["dve"], 1)
                n[0] += 1
                ve.wait_ge(S["dve"], n[0])

            def stats(g, b):
                ve.wait_ge(S["x_landed"], g + 1)
                for j in range(GT):
                    ve.bn_stats(st6[:, b, j, :], xin[:, ds(g * GT + j, 1), :].rearrange("p a c -> p (a c)"))
                ve.drain()
                for j in range(GT):
                    ve.bn_aggr(mv[:, b, j, :], st6[:, b, j, :])
                ve.drain()
                ve.tensor_scalar(veps[:, b, :], mv[:, b, :, 1], 1e-5, None, ALU.add).then_inc(S["stats"], 1)

            def normalise(g, b, first=False):
                ve.wait_ge(S["sd_ready"], g + 1)
                ve.reciprocal(rs0[:, :], sd[:, b, :])
                ve.drain()
                ve.tensor_tensor(rs1[:, :], rs0[:, :], rs0[:, :], ALU.mult)
                ve.drain()
                ve.tensor_tensor(rs2[:, :], rs1[:, :], veps[:, b, :], ALU.mult)
                ve.drain()
                ve.tensor_scalar(rs1[:, :], rs2[:, :], -0.5, 1.5, ALU.mult, ALU.add)
                ve.drain()
                ve.tensor_tensor(rstd[:, :], rs0[:, :], rs1[:, :], ALU.mult)
                ve.drain()
                if not first:
                    ve.wait_ge(S["lo_ready"], g - 1)
                for j in range(GT):
                    last = ve.tensor_scalar(xn[:, b, j, :], xin[:, ds(g * GT + j, 1), :].rearrange("p a c -> p (a c)"),
                                            mv[:, b, j, 0:1], rstd[:, j:j + 1], ALU.subtract, ALU.mult)
                last.then_inc(S["xn_ready"], 1)

            stats(0, 0)
            stats(1, 1)
            normalise(0, 0, first=True)
            stats(2, 0)
            normalise(1, 1, first=True)
            with ve.Fori(1, NG // 2 - 1) as r:
                stats(r * 2 + 1, 1)
                normalise(r * 2, 0)
                stats(r * 2 + 2, 0)
                normalise(r * 2 + 1, 1)
            stats(NG - 1, 1)
            normalise(NG - 2, 0)
            normalise(NG - 1, 1)

            ve.wait_ge(S["consts"], NCONST)
            ve.wait_ge(S["wsmall_in"], 16 * NW)
            ve.wait_ge(S["biases_in"], 16 * 8)
            step(ve.tensor_scalar(rw[:, 0, :], rw_raw[:, :], RS, None, ALU.mult))
            ve.scalar_tensor_tensor(rw[:, 1, :], rw_raw[:, :], RS, rw[:, 0, :], ALU.mult, ALU.subtract).then_inc(S["rw_ready"], 1)
            ve.tensor_copy(bk_wide[:, :], bqk[:, 1:2].to_broadcast([P, C]))
            ve.scalar_tensor_tensor(rblk[:, :].rearrange("p (h d) -> p h d", d=HD),
                                    r_rep[:, :].unsqueeze(1).to_broadcast([P, HEADS, HD]), WS / HD ** 0.5, blk[:, :, :],
                                    ALU.mult, ALU.mult).then_inc(S["setup_dve"], 1)
            ve.tensor_scalar(negblk[:, :], blk[:, :, :].rearrange("p h d -> p (h d)"), -1.0, None, ALU.mult)
            ve.tensor_scalar(bv_bc[:, :], bv_bc[:, :], WS, None, ALU.mult)
            step(ve.tensor_scalar(WH[:, 0:3, :], w3[:, :, :], WS, None, ALU.mult))
            step(ve.scalar_tensor_tensor(WL[:, 0:3, :], w3[:, :, :], WS, WH[:, 0:3, :], ALU.mult, ALU.subtract))
            ve.wait_ge(S["setup_pe"], 1)
            step(ve.tensor_copy(WH[:, 3:5, :].rearrange("p a c -> p (a c)"), bank[6][:, 0:2 * C]))
            step(ve.tensor_tensor(WL[:, 3:5, :].rearrange("p a c -> p (a c)"), bank[6][:, 0:2 * C],
                                  WH[:, 3:5, :].rearrange("p a c -> p (a c)"), ALU.subtract))
            step(ve.tensor_copy(kb_hi[:, :], bank[7][:, 0:C]))
            ve.tensor_copy(kb_rows[0:1, :], kb_hi[0:1, :])
            ve.tensor_tensor(kb_rows[32:33, :], bank[7][32:33, 0:C], kb_hi[32:33, :], ALU.subtract)
            ve.tensor_scalar(bpq[:, :], bank[7][:, C:C + 1], 1.0 / WS, None, ALU.mult).then_inc(S["setup_dve"], 1)
            for rows, raw, hi, n0, scale in ((b1_rows, b1_raw, b1_hi, FC, WS), (b2_rows, b2_raw, b2_hi, 1, WS * WS)):
                flat = "p e f -> p (e f)"
                ve.tensor_scalar(rows[0:n0, :], raw[0:n0, :, :].rearrange(flat), scale, None, ALU.mult)
                step(ve.tensor_scalar(hi[32:32 + n0, :, :], raw[32:32 + n0, :, :], scale, None, ALU.mult))
                step(ve.scalar_tensor_tensor(rows[32:32 + n0, :], raw[32:32 + n0, :, :].rearrange(flat), scale,
                                             hi[32:32 + n0, :, :].rearrange(flat), ALU.mult, ALU.subtract))

            def over_e(a):
                return a.unsqueeze(2).to_broadcast([P, NJ, E])

            def first_max(src, m, pick):
                step(ve.tensor_reduce(m[:, :], src[:, :, :], AX.X, ALU.max))
                step(ve.tensor_tensor(eq[:, :, :], src[:, :, :], over_e(m[:, :]), ALU.is_equal))
                step(ve.tensor_tensor(sc[:, :, :], eq[:, :, :], rank8[:, :].unsqueeze(1).to_broadcast([P, NJ, E]), ALU.mult))
                step(ve.tensor_reduce(mx[:, :], sc[:, :, :], AX.X, ALU.max))
                step(ve.tensor_tensor(pick[:, :, :], sc[:, :, :], over_e(mx[:, :]), ALU.is_equal))

            ve.wait_ge(S["logits"], 1)
            step(ve.tensor_copy(lg[:, :, :].rearrange("p j e -> p (j e)"), bank[2][:, 0:NJ * E]))
            first_max(lg, m1, pick1)
            step(ve.scalar_tensor_tensor(lg2[:, :, :], pick1[:, :, :], -1e30, lg[:, :, :], ALU.mult, ALU.add))
            first_max(lg2, m2, pick2)
            ve.tensor_tensor(took[:, :, :].rearrange("p e j -> p j e"), pick1[:, :, :], pick2[:, :, :], ALU.add).then_inc(S["took_ready"], 1)
            ve.tensor_tensor(dlt[:, :, :], lg[:, :, :], over_e(m1[:, :]), ALU.subtract).then_inc(S["exp_in"], 1)
            ve.tensor_tensor(d2[:, :], m2[:, :], m1[:, :], ALU.subtract).then_inc(S["exp_in"], 1)
            ve.wait_ge(S["counts"], 1)
            step(ve.tensor_copy(tot[:, :, :].rearrange("p e j -> p (e j)"), bank[4][:, 0:E * NJ]))
            step(ve.tensor_tensor_scan(run[:, :, :].rearrange("p e j -> p (e j)"), ones_row[:, :],
                                       tot[:, :, :].rearrange("p e j -> p (e j)"), 0.0, ALU.mult, ALU.add))
            ve.tensor_tensor(exc[:, :, :], run[:, :, :], tot[:, :, :], ALU.subtract)
            step(ve.tensor_reduce(cnt[:, :], tot[:, :, :], AX.X, ALU.add))
            step(ve.tensor_scalar(cnt_i[:, :], cnt[:, :], float(P - 1), None, ALU.add))
            step(ve.tensor_scalar(nt_i[:, :], cnt_i[:, :], 7, None, ALU.arith_shift_right))
            step(ve.tensor_copy(nt_f[:, :], nt_i[:, :]))
            step(ve.tensor_tensor_scan(end_t[:, :], ones_row[:, 0:E], nt_f[:, :], 0.0, ALU.mult, ALU.add))
            step(ve.tensor_tensor(base[:, :], end_t[:, :], nt_f[:, :], ALU.subtract))
            step(ve.scalar_tensor_tensor(offs[:, :], base[:, :], float(P), exc[:, :, 0], ALU.mult, ALU.subtract))
            step(ve.tensor_tensor(pos[:, :, :].rearrange("p e j -> p (e j)"), bank[3][:, 0:E * NJ],
                                  exc[:, :, :].rearrange("p e j -> p (e j)"), ALU.add))
            step(ve.tensor_tensor(pos2[:, :, :], pos[:, :, :], offs[:, :].unsqueeze(2).to_broadcast([P, E, NJ]), ALU.add))
            for k, pick in enumerate((pick1, pick2)):
                step(ve.tensor_tensor(ppick[:, :, :], pick[:, :, :], pos2[:, :, :].rearrange("p e j -> p j e"), ALU.mult))
                step(ve.tensor_reduce(slot[:, k * NJ:(k + 1) * NJ], ppick[:, :, :], AX.X, ALU.add))
            step(ve.tensor_copy(slot_i[:, :], slot[:, :]))
            ve.tensor_scalar(lo_i[:, :], slot_i[:, :], P - 1, None, ALU.bitwise_and)
            step(ve.tensor_scalar(hi_i[:, :], slot_i[:, :], 7, None, ALU.arith_shift_right))
            ve.tensor_copy(lo_f[:, :], lo_i[:, :])
            step(ve.tensor_copy(hi_f[:, :], hi_i[:, :]))

            def onehots(i, u):
                ve.tensor_scalar(oh_lo[:, u, :], iota_e[:, :], lo_f[:, ds(i, 1)], None, ALU.is_equal)
                ve.tensor_scalar(oh_hi[:, u, 0:NT], iota_e[:, 0:NT], hi_f[:, ds(i, 1)], p1col[:, 0:1], ALU.is_equal, ALU.mult)
                ve.tensor_scalar(oh_hi[:, u, NT:2 * NT], iota_e[:, 0:NT], hi_f[:, ds(i, 1)], jcol[:, ds(i, 1)],
                                 ALU.is_equal, ALU.mult).then_inc(S["onehot"], 1)

            for u in range(4):
                onehots(u, u)
            with ve.Fori(1, 2 * NJ // 4) as r:
                for u in range(4):
                    ve.wait_ge(S["perm_used"], r * 4 + u - 3)
                    onehots(r * 4 + u, u)
            step(ve.tensor_tensor(cmp_t[:, :, :], end_t[:, :].unsqueeze(1).to_broadcast([P, NT, E]),
                                  iota_t[:, :].unsqueeze(2).to_broadcast([P, NT, E]), ALU.is_le))
            step(ve.tensor_reduce(et_f[:, :], cmp_t[:, :, :], AX.X, ALU.add))
            ve.tensor_scalar(et_i[:, :], et_f[:, :], float(E - 1), None, ALU.min).then_inc(S["ids_ready"], 1)
            ve.wait_ge(S["perm"], 1)
            step(ve.tensor_copy(ip[:, :], bank[5][:, 0:NT]))
            step(ve.scalar_tensor_tensor(idf[:, :], bank[5][:, NT:2 * NT], float(P), ip[:, :], ALU.mult, ALU.add))
            step(ve.tensor_scalar(gidf[:, :], idf[:, :], -1.0, 0.0, ALU.add, ALU.max))
            step(ve.tensor_copy(gid_i[:, :], gidf[:, :]))
            ve.tensor_scalar(gid[:, :], gid_i[:, :], T - 1, None, ALU.bitwise_and).then_inc(S["ids_ready"], 1)
            step(ve.scalar_tensor_tensor(inv[:, :], idf[:, :], 0.0, waste[:, :], ALU.is_equal, ALU.mult))
            step(ve.tensor_tensor(sid_f[:, :], inv[:, :], idf[:, :], ALU.add))
            ve.tensor_scalar(sid[:, :], sid_f[:, :], -1.0, None, ALU.add).then_inc(S["ids_ready"], 1)
            ve.wait_ge(S["exp_out"], 2)
            step(ve.tensor_reduce(ssum[:, :], ex[:, :, :], AX.X, ALU.add))
            step(ve.reciprocal(pr1[:, :], ssum[:, :]))
            step(ve.tensor_tensor(pr2[:, :], ex2[:, :], pr1[:, :], ALU.mult))
            step(ve.scalar_tensor_tensor(den[:, :], pr2[:, :], 1e-9, pr1[:, :], ALU.add, ALU.add))
            step(ve.reciprocal(rden[:, :], den[:, :]))
            ve.tensor_tensor(gate1[:, :], pr1[:, :], rden[:, :], ALU.mult)
            step(ve.tensor_tensor(gate2[:, :], pr2[:, :], rden[:, :], ALU.mult))

            def values(g):
                ve.wait_ge(S["v_proj"], g + 1)
                ve.tensor_tensor(vv[:, :, :], bank[3][:, :].rearrange("p (j c) -> p j c", j=GT),
                                 bv_bc[:, :].unsqueeze(1).to_broadcast([P, GT, C]), ALU.add).then_inc(S["v_ready"], 1)

            def key_values(g):
                ve.wait_ge(S["kv_sum"], g + 1)
                ve.scalar_tensor_tensor(kvm[:, :, :], bank[4][:, 0:2 * C].rearrange("p (b c) -> p b c", b=2), 1.0 / WS,
                                        blk[:, :, :].rearrange("p h d -> p (h d)").unsqueeze(1).to_broadcast([P, 2, C]),
                                        ALU.mult, ALU.mult).then_inc(S["kv_ready"], 1)

            def weigh(g):
                ve.wait_ge(S["nums"], g + 1)
                for h in range(2):
                    ve.tensor_scalar(zz[:, h, :, :], bank[5 + h][:, 0:288].rearrange("p (a c) -> p a c", a=2)[:, :, C:],
                                     1e-8, None, ALU.add)
                ve.drain()
                ve.reciprocal(zr[:, :, :, :], zz[:, :, :, :])
                ve.drain()
                for a in range(GT):
                    last = ve.tensor_tensor(oo[:, a, :].rearrange("p (h d) -> p h d", d=HD),
                                            bank[5 + a // 2][:, a % 2 * 144:a % 2 * 144 + C].rearrange("p (h d) -> p h d", d=HD),
                                            zr[:, a // 2, a % 2, :].unsqueeze(2).to_broadcast([P, HEADS, HD]), ALU.mult)
                last.then_inc(S["o_ready"], 1)

            def residual(g):
                ve.wait_ge(S["wo_out"], g + 1)
                ve.tensor_tensor(xin[:, ds(g * GT, GT), :], bank[7][:, :].rearrange("p (j c) -> p j c", j=GT),
                                 xin[:, ds(g * GT, GT), :], ALU.add).then_inc(S["acc_ready"], 1)

            def dve_group(g, first=False):
                values(g)
                if not first:
                    residual(g - 1)
                key_values(g)
                weigh(g)

            ve.wait_ge(S["wsplit_hi"], 1)
            ve.scalar_tensor_tensor(w1l[:, :], wraw[:, :], WS, w1h[:, :], ALU.mult, ALU.subtract).then_inc(S["w_split"], 1)
            ve.wait_ge(S["wsplit_hi"], 2)
            ve.scalar_tensor_tensor(w2l[:, :], wraw2[:, :], WS, w2h[:, :], ALU.mult, ALU.subtract).then_inc(S["w_split"], 1)
            ve.wait_ge(S["xb_ready"], NG)
            dve_group(0, first=True)
            with ve.Fori(1, NG) as g:
                dve_group(g)
            residual(NG - 1)

            def rows(t, b):
                ve.wait_ge(S["slots_tr"], t + 1)
                ve.tensor_copy(xgT[:, b, :, :].rearrange("p s c -> p (s c)"), bank[b][:, 0:P].bitcast(F16)).then_inc(S["slots_ready"], 1)

            def low(t, b):
                ve.wait_ge(S["hh_ready"], t + 1)
                ve.scalar_tensor_tensor(hl[:, b, :], bank[2 + b][:, :], 0.0, hh[:, b, :], ALU.max, ALU.subtract).then_inc(S["hl_ready"], 1)

            rows(0, 0)
            rows(1, 1)
            low(0, 0)
            with ve.Fori(0, NT // 2 - 1) as r:
                for b in range(2):
                    rows(r * 2 + b + 2, b)
                    low(r * 2 + b + 1, 1 - b)
            low(NT - 1, 1)

            for i in range(4):
                ve.wait_ge(y_in[i], 32)
                with ve.Fori(i * NJ // 4, (i + 1) * NJ // 4) as j:
                    acc = xin[:, ds(j, 1), :].rearrange("p a c -> p (a c)")
                    ve.scalar_tensor_tensor(acc, wraw[:, ds(j * C, C)], gate1[:, ds(j, 1)], acc, ALU.mult, ALU.add)
                    ve.drain()
                    ve.scalar_tensor_tensor(acc, wraw2[:, ds(j * C, C)], gate2[:, ds(j, 1)], acc, ALU.mult, ALU.add).then_inc(S["summed"], 1)

        @block.tensor
        def _(pe):
            def mm(o, l, r, start=False, stop=False):
                return pe.matmul(o, l, r, start=start, stop=stop, skip_group_check=True)

            def transposes(g, b, first=False):
                pe.wait_ge(S["hi_ready"], g + 1)
                pe.wait_ge(S["lo_ready"], g + 1)
                if not first:
                    pe.wait_ge(S["xT_ready"], g - 1)
                o = bank[b][:, :].bitcast(F16)
                for s in range(2):
                    for j in range(GT):
                        at = (s * GT + j) * P
                        last = pe.transpose(o[:, at:at + P], xs[:, ds(g * GT + j, 1), s, :].rearrange("p a c -> p (a c)"), id16[:, :])
                last.then_inc(S["xT_tr"], 1)

            def router(g):
                pe.wait_ge(S["xT_ready"], g + 1)
                for j in range(GT):
                    o = bank[2][:, ds((g * GT + j) * E, E)]
                    hi = xT[:, 0, ds(g * GN + j * P, P)]
                    mm(o, hi, rw[:, 0, :], start=isinstance(g, int) and g == 0 and j == 0)
                    mm(o, hi, rw[:, 1, :])
                    last = mm(o, xT[:, 1, ds(g * GN + j * P, P)], rw[:, 0, :], stop=True)
                return last

            pe.wait_ge(S["consts"], NCONST)
            transposes(0, 0, first=True)
            transposes(1, 1, first=True)
            with pe.Fori(1, NG // 2) as r:
                transposes(r * 2, 0)
                transposes(r * 2 + 1, 1)
            pe.wait_ge(S["rw_ready"], 1)
            router(0)
            with pe.Fori(1, NG - 1) as g:
                router(g)
            router(NG - 1).then_inc(S["logits"], 1)
            pe.wait_ge(S["setup_dve"], 1)
            mm(bank[6][:, 0:C], wnat[:, 0, :], rblk[:, :], start=True, stop=True)
            mm(bank[6][:, C:2 * C], wnat[:, 1, :], rblk[:, :], start=False, stop=True)
            mm(bank[7][:, 0:C], bk_wide[:, :], rblk[:, :], start=True, stop=True)
            mm(bank[7][:, C:C + 1], rblk[:, :], bqk[:, 0:1], start=False, stop=True).then_inc(S["setup_pe"], 1)
            pe.wait_ge(S["took_ready"], 1)
            flat = took[:, :, :].rearrange("p e j -> p (e j)")
            mm(bank[3][:, 0:E * NJ], before[:, :], flat, start=True, stop=True)
            mm(bank[4][:, 0:E * NJ], onesb[:, :], flat, start=True, stop=True).then_inc(S["counts"], 1)

            def place(i, u, first=False, last=False):
                pe.wait_ge(S["onehot"], i + 1)
                m = mm(bank[5][:, 0:2 * NT], oh_lo[:, u, :], oh_hi[:, u, :], start=first, stop=last)
                m.then_inc(S["perm_used"], 1)

            for u in range(4):
                place(u, u, first=(u == 0))
            with pe.Fori(1, 2 * NJ // 4 - 1) as r:
                for u in range(4):
                    place(r * 4 + u, u)
            for u in range(4):
                i = 2 * NJ - 4 + u
                pe.wait_ge(S["onehot"], i + 1)
                m = mm(bank[5][:, 0:2 * NT], oh_lo[:, u, :], oh_hi[:, u, :], stop=(u == 3))
                m.then_inc(S["perm_used"] if u < 3 else S["perm"], 1)

            def project(g, w):
                for n_, (a, b) in enumerate(((WH, 0), (WH, 1), (WL, 0))):
                    m = mm(bank[0][:, :], a[:, w, :], xT[:, b, ds(g * GN, GN)], start=(n_ == 0), stop=(n_ == 2))
                return m

            def project_q(g, first=False):
                if not first:
                    pe.wait_ge(S["k_sq"], g)
                project(g, Q).then_inc(S["q_proj"], 1)

            def project_k(g):
                pe.wait_ge(S["q_sq"], g + 1)
                project(g, K).then_inc(S["k_proj"], 1)

            def exponents_a(g, first=False):
                if not first:
                    pe.wait_ge(S["q_feat"], g)
                for n_, (a, b) in enumerate(((WH, 0), (WH, 1), (WL, 0))):
                    mm(bank[1][:, :], a[:, PQ, :], xT[:, b, ds(g * GN, GN)], start=(n_ == 0))
                if not first:
                    pe.wait_ge(S["k_feat"], g)
                for j in range(GT):
                    o = bank[2][:, j * P:(j + 1) * P]
                    hi, lo = (xT[:, b, ds(g * GN + j * P, P)] for b in range(2))
                    mm(o, hi, WH[:, PK, :], start=(j == 0))
                    mm(o, hi, WL[:, PK, :])
                    mm(o, lo, WH[:, PK, :])
                    mm(o, ones16[:, :], kb_rows[:, :])
                if not first:
                    pe.wait_ge(S["v_ready"], g)
                for j in range(GT):
                    o = bank[3][:, j * P:(j + 1) * P]
                    hi, lo = (xT[:, b, ds(g * GN + j * P, P)] for b in range(2))
                    mm(o, hi, WH[:, V, :], start=(j == 0))
                    mm(o, hi, WL[:, V, :])
                    m = mm(o, lo, WH[:, V, :], stop=True)
                m.then_inc(S["v_proj"], 1)

            def exponents_b(g):
                pe.wait_ge(S["q_sq"], g + 1)
                mm(bank[1][:, :], negblk[:, :], q2[:, :], stop=True).then_inc(S["q_expo"], 1)
                pe.wait_ge(S["k_sq"], g + 1)
                for j in range(GT):
                    m = mm(bank[2][:, j * P:(j + 1) * P], k2[:, j * P:(j + 1) * P], negblk[:, :], stop=True)
                m.then_inc(S["k_expo"], 1)

            def sums(g, first=False):
                pe.wait_ge(S["k_feat"], g + 1)
                pe.wait_ge(S["v_ready"], g + 1)
                if not first:
                    pe.wait_ge(S["kv_ready"], g)
                for b in range(2):
                    for s in range(2):
                        m = mm(bank[4][:, b * C:(b + 1) * C], kf[:, 2 * b + s, :], vv[:, 2 * b + s, :],
                               start=(b == 0 and s == 0), stop=(s == 1))
                m.then_inc(S["kv_sum"], 1)

            def numerators(g, first=False):
                pe.wait_ge(S["q_feat"], g + 1)
                pe.wait_ge(S["kv_ready"], g + 1)
                if not first:
                    pe.wait_ge(S["o_ready"], g)
                for a in range(GT):
                    o = bank[5 + a // 2]
                    at = a % 2 * 144
                    l = qf[:, a * P:(a + 1) * P]
                    mm(o[:, at:at + C], l, kvm[:, a // 2, :], start=(a % 2 == 0), stop=True)
                    m = mm(o[:, at + C:at + C + HEADS], l, headof[:, :], stop=True)
                m.then_inc(S["nums"], 1)

            def turn(g, first=False):
                pe.wait_ge(S["o_ready"], g + 1)
                if not first:
                    pe.wait_ge(S["acc_ready"], g)
                for a in range(GT):
                    m = pe.transpose(bank[7][:, a * P:(a + 1) * P], oo[:, a, :], id32[:, :])
                m.then_inc(S["o_trans"], 1)

            def project_out(g):
                pe.wait_ge(S["oT_ready"], g + 1)
                for a in range(GT):
                    m = mm(bank[7][:, a * P:(a + 1) * P], oT[:, a * P:(a + 1) * P], wo_sb[:, :], start=(a == 0), stop=True)
                m.then_inc(S["wo_out"], 1)

            def pe_group(g, first=False, last=False):
                exponents_a(g, first)
                if not first:
                    turn(g - 1, first=isinstance(g, int) and g == 1)
                exponents_b(g)
                if not last:
                    project_q(g + 1)
                if not first:
                    project_out(g - 1)
                if not last:
                    project_k(g + 1)
                sums(g, first)
                numerators(g, first)

            pe.wait_ge(S["setup_dve"], SETUP_BPQ)
            pe.wait_ge(S["xs_stored"], 16 * NG)
            project_q(0, first=True)
            project_k(0)
            pe_group(0, first=True)
            pe_group(1)
            with pe.Fori(2, NG - 1) as g:
                pe_group(g)
            pe_group(NG - 1, last=True)
            turn(NG - 1)
            project_out(NG - 1)

            def slots(t, b, first=False):
                pe.wait_ge(S["gathered"], t + 1)
                if not first:
                    pe.wait_ge(S["slots_ready"], t - 1)
                o = bank[b][:, 0:P].bitcast(F16)
                for s in range(2):
                    m = pe.transpose(o[:, s * P:(s + 1) * P], xg[:, ds(t, 1), s * C:(s + 1) * C].rearrange("p a c -> p (a c)"), id16[:, :])
                m.then_inc(S["slots_tr"], 1)

            def expert(t):
                return pe.value_load(et_i[0:1, ds(t, 1)], min_val=0, max_val=E - 1)

            def layer1(t, b, first=False):
                e = expert(t)
                pe.wait_ge(S["slots_ready"], t + 1)
                if not first:
                    pe.wait_ge(S["hl_ready"], t - 1)
                mm(bank[2 + b][:, :], b1_rows[:, ds(e * P, P)], chunk_of[:, :, :].rearrange("p f n -> p (f n)"), start=True)
                for c in range(FC):
                    o = bank[2 + b][:, c * P:(c + 1) * P]
                    h = w1h[:, ds(e * F + c * P, P)]
                    mm(o, h, xgT[:, b, 0, :])
                    mm(o, h, xgT[:, b, 1, :])
                    m = mm(o, w1l[:, ds(e * F + c * P, P)], xgT[:, b, 0, :], stop=(c == FC - 1))
                m.then_inc(S["h_ready"], 1)

            def layer2(t, b, first=False):
                e = expert(t)
                if not first:
                    pe.wait_ge(S["y_out"], t - 1)
                o = bank[4 + b][:, 0:C]
                mm(o, ones16[:, :], b2_rows[:, ds(e * C, C)], start=True)
                pe.wait_ge(S["hh_ready"], t + 1)
                for c in range(FC):
                    mm(o, hh[:, b, c * P:(c + 1) * P], w2h[:, ds(e * F + c * C, C)])
                    mm(o, hh[:, b, c * P:(c + 1) * P], w2l[:, ds(e * F + c * C, C)])
                pe.wait_ge(S["hl_ready"], t + 1)
                for c in range(FC):
                    m = mm(o, hl[:, b, c * P:(c + 1) * P], w2h[:, ds(e * F + c * C, C)], stop=(c == FC - 1))
                m.then_inc(S["y_ready"], 1)

            pe.wait_ge(S["w_split"], 2)
            pe.wait_ge(S["acc_ready"], NG)
            pe.wait_ge(S["ids_ready"], 1)
            slots(0, 0, first=True)
            slots(1, 1, first=True)
            layer1(0, 0, first=True)
            for b in range(2):
                slots(2 + b, b)
                layer1(1 + b, 1 - b, first=(b == 0))
                layer2(b, b, first=True)
            with pe.Fori(1, NT // 2 - 1) as r:
                for b in range(2):
                    slots(r * 2 + b + 2, b)
                    layer1(r * 2 + b + 1, 1 - b)
                    layer2(r * 2 + b, b)
            layer1(NT - 1, 1)
            layer2(NT - 2, 0)
            layer2(NT - 1, 1)


NCONST = 27
SETUP_BPQ = 2


def kernel(L0_attn_x, L0_attn_Wq, L0_attn_bq, L0_attn_Wk, L0_attn_bk, L0_attn_Wv, L0_attn_bv, L0_attn_Wo, L0_attn_bo,
           L0_attn_R, L0_ffn_router_w, L0_ffn_w1, L0_ffn_b1, L0_ffn_w2, L0_ffn_b2):
    import numpy as np
    import concourse.bacc as bacc
    from concourse.bass_utils import run_bass_kernel_spmd

    a = np.asarray
    w1, w2 = a(L0_ffn_w1), a(L0_ffn_w2)
    arrays = {
        "x": a(L0_attn_x),
        "wq": a(L0_attn_Wq), "wk": a(L0_attn_Wk),
        "wqT": a(L0_attn_Wq).T, "wkT": a(L0_attn_Wk).T, "wvT": a(L0_attn_Wv).T, "woT": a(L0_attn_Wo).T,
        "bq": a(L0_attn_bq)[:, None], "bk": a(L0_attn_bk)[:, None], "bv": a(L0_attn_bv), "bo": a(L0_attn_bo),
        "R": np.tile(a(L0_attn_R), (HEADS, 1)),
        "rwT": a(L0_ffn_router_w).T,
        "w1T": w1.transpose(2, 0, 1).reshape(C, E * F),
        "b1": a(L0_ffn_b1).reshape(E, FC, P).transpose(1, 0, 2),
        "w2T": w2.reshape(E, C, FC, P).transpose(3, 0, 2, 1).reshape(P, E * FC * C),
        "b2": a(L0_ffn_b2)[None],
    }
    arrays = {f"in_{k}": np.ascontiguousarray(v) for k, v in arrays.items()}
    nc = bacc.Bacc("TRN2", target_bir_lowering=False, num_devices=1)
    args = [nc.dram_tensor(k, v.shape, mybir.dt.from_np(v.dtype), kind="ExternalInput").ap() for k, v in arrays.items()]
    result = nc.dram_tensor("out_0", (16, 256, 128), F32, kind="ExternalOutput").ap()
    build(nc, *args, result)
    r = run_bass_kernel_spmd(nc, [arrays], core_ids=[0])
    return r.results[0]["out_0"]
```

```python
from contextlib import ExitStack

import concourse.bass as bass
from concourse import mybir

F32 = mybir.dt.float32
F16 = mybir.dt.float16
BF16 = mybir.dt.bfloat16
I32 = mybir.dt.int32
ALU = mybir.AluOpType
ACT = mybir.ActivationFunctionType
AX = mybir.AxisListType
ds = bass.ds

P = 128
C = 128
HEADS, HD = 16, 8
E, F = 8, 512
FC = F // P
WS = 16.0
RS = 1024.0
Q, K, V, PQ, PK = range(5)


def build(nc, x, wq, wk, wqT, wkT, wvT, woT, bq, bk, bv, bo, R, rwT, w1T, b1, w2T, b2, out):
    T = x.shape[0] * x.shape[1]
    NJ = T // P
    GT = 4
    GN = GT * P
    NG = NJ // GT
    NT = 2 * T // P + E
    PAIRS = 2 * T
    assert NT % 4 == 0 and x.shape[1] == 2 * P

    x_rows = x.rearrange("b n c -> (b n) c")
    out_rows = out.rearrange("b n c -> (b n) c")
    RW = 2 * C + 8
    slot_dram = nc.dram_tensor("slot_dram", [NT * P, RW], F16).ap()
    y_dram = nc.dram_tensor("y_dram", [PAIRS + 4 * P, C], F32).ap()

    with ExitStack() as ctx:
        def sb(name, shape, dt=F32):
            return ctx.enter_context(nc.sbuf_tensor(name, shape, dt))

        def sem(name):
            return ctx.enter_context(nc.semaphore(name))

        bank = [ctx.enter_context(nc.psum_tensor(f"bank{i}", [P, 512], F32)) for i in range(8)]

        xin = sb("xin", [P, NJ, C])
        xs = sb("xs", [P, NJ, RW], F16)
        xT = sb("xT", [P, 2, T], F16)
        xg = sb("xg", [P, NT, RW], F16)
        WSET = 4 * F + P + C
        wsets = sb("wsets", [P, E * WSET], F16)
        wv = wsets[:, :].rearrange("p (e n) -> p e n", e=E)
        w1h, w1l, w2h, w2l = (wv[:, :, i * F:(i + 1) * F] for i in range(4))
        b1_rows = wv[:, :, 4 * F:4 * F + P]
        b2_rows = wv[:, :, 4 * F + P:]
        wraw = sb("wraw", [P, E * F])
        wraw2 = sb("wraw2", [P, E * F])
        early = xg[:, :, :].rearrange("p t c -> p (t c)")
        b1_raw = early[:, 0:2048].bitcast(F32).rearrange("p (e f) -> p e f", e=E)
        b2_raw = early[:, 2048:4096].bitcast(F32).rearrange("p (e f) -> p e f", e=E)
        b1_hi = early[:, 4096:5120].rearrange("p (e f) -> p e f", e=E)
        b2_hi = early[:, 5120:6144].rearrange("p (e f) -> p e f", e=E)
        fill = early[:, 6144:6144 + 4 * RW].rearrange("p (u c) -> p u c", u=4)
        wnat = sb("wnat", [P, 2, C])
        w3 = sb("w3", [P, 3, C])
        wo_sb = sb("wo_sb", [P, C])
        WH = sb("WH", [P, 5, C], F16)
        WL = sb("WL", [P, 5, C], F16)
        r_rep = sb("r_rep", [P, HD])
        rblk = sb("rblk", [P, C])
        rw_raw = sb("rw_raw", [P, E])
        rw = sb("rw", [P, 2, E], F16)
        bqk = sb("bqk", [P, 2])
        bk_wide = sb("bk_wide", [P, C])
        bpq = sb("bpq", [P, 1])
        bv_bc = sb("bv_bc", [P, C])
        bo_bc = sb("bo_bc", [P, C])
        kb_rows = sb("kb_rows", [P, C], F16)
        kb_hi = sb("kb_hi", [P, C], F16)
        id16 = sb("id16", [P, P], F16)
        ones16 = sb("ones16", [P, P], F16)
        onesb = sb("onesb", [P, P], BF16)
        before = sb("before", [P, P], BF16)
        blk = sb("blk", [P, HEADS, HD])
        negblk = sb("negblk", [P, C])
        chunk_of = sb("chunk_of", [P, FC, P], F16)
        rank8 = sb("rank8", [P, E])
        iota_t = sb("iota_t", [P, NT + 4])
        t_const = sb("t_const", [P, NJ], I32)
        ones_row = sb("ones_row", [P, E * NJ])
        HJ = NJ // 2
        st6 = sb("st6", [P, HJ, 6])
        mv = sb("mv", [P, HJ, 2])
        veps = sb("veps", [P, HJ])
        sd = sb("sd", [P, HJ])
        rs0 = sb("rs0", [P, HJ])
        rs1 = sb("rs1", [P, HJ])
        rs2 = sb("rs2", [P, HJ])
        rstd = sb("rstd", [P, HJ])
        xn = sb("xn", [P, NG // 2, GT, C])
        lg = sb("lg", [P, NJ, E])
        m1 = sb("m1", [P, NJ])
        m2 = sb("m2", [P, NJ])
        eq = sb("eq", [P, NJ, E])
        sc = sb("sc", [P, NJ, E])
        mx = sb("mx", [P, NJ])
        pick1 = sb("pick1", [P, NJ, E])
        pick2 = sb("pick2", [P, NJ, E])
        lg2 = sb("lg2", [P, NJ, E])
        dlt = sb("dlt", [P, NJ, E])
        d2 = sb("d2", [P, NJ])
        ex = sb("ex", [P, NJ, E])
        ex2 = sb("ex2", [P, NJ])
        ssum = sb("ssum", [P, NJ])
        pr1 = sb("pr1", [P, NJ])
        pr2 = sb("pr2", [P, NJ])
        den = sb("den", [P, NJ])
        rden = sb("rden", [P, NJ])
        gate1 = sb("gate1", [P, NJ])
        gate2 = sb("gate2", [P, NJ])
        took = sb("took", [P, E, NJ], BF16)
        tot = sb("tot", [P, E, NJ])
        run = sb("run", [P, E, NJ])
        exc = sb("exc", [P, E, NJ])
        cnt = sb("cnt", [P, E])
        cnt_i = sb("cnt_i", [P, E], I32)
        nt_i = sb("nt_i", [P, E], I32)
        nt_f = sb("nt_f", [P, E])
        end_t = sb("end_t", [P, E])
        base = sb("base", [P, E])
        offs = sb("offs", [P, E])
        pos = sb("pos", [P, E, NJ])
        pos2 = sb("pos2", [P, E, NJ])
        ppick = sb("ppick", [P, NJ, E])
        slot = sb("slot", [P, 2 * NJ])
        slot_i = sb("slot_i", [P, 2 * NJ], I32)
        cmp_t = sb("cmp_t", [P, NT + 4, E])
        et_f = sb("et_f", [P, NT + 4])
        et_i = sb("et_i", [P, NT + 4], I32)
        q2, k2, qf, kf2 = (xn[:, i, :, :].rearrange("p j c -> p (j c)") for i in range(4))
        vv2, rz, oT = (sb(f"att{i}", [P, GN]) for i in range(3))
        zz = sb("zz", [P, GN])
        kf, vv = (a.rearrange("p (j c) -> p j c", j=GT) for a in (kf2, vv2))
        kvm = sb("kvm", [P, 2, C])
        free2 = xT[:, :, :].rearrange("p s n -> p (s n)")
        xgT = free2[:, 0:4 * P].rearrange("p (b s n) -> p b s n", b=2, s=2)
        hh = free2[:, 1024:1024 + 2 * F].rearrange("p (b f) -> p b f", b=2)
        hl = free2[:, 2048:2048 + 2 * F].rearrange("p (b f) -> p b f", b=2)
        yb = free2[:, 3072:3072 + 8 * C].bitcast(F32).rearrange("p (b c) -> p b c", b=4)
        xs_free = xs[:, :, :].rearrange("p j c -> p (j c)")
        wset = [xs_free[:, i * WSET:(i + 1) * WSET] for i in range(3)] + [free2[:, 4096:4096 + WSET]]

        names = """consts rw_in wsmall_in biases_in w1_in w2_in filled
            x_landed stats sd_ready xn_ready hi_ready lo_ready xb_ready xT_tr xT_ready
            rw_ready rblk_ready folded bpq_ready biases_split w_hi w_lo
            logits counts took_ready exp_in exp_out slots_known experts_known dve
            q_proj k_proj q_expo k_expo v_proj kv_sum nums dens wo_out
            q_sq k_sq q_feat k_feat v_ready kv_ready dens_read oT_ready acc_ready
            rows_landed slots_tr slots_ready set_ready h_ready hh_ready hl_ready y_ready y_out y_free
            summed stored""".split()
        S = {n: sem(n) for n in names}
        x_in = [sem(f"x_in{i}") for i in range(4)]
        place_in = [sem(f"place_in{i}") for i in range(4)]
        scatter_in = [sem(f"scatter_in{i}") for i in range(4)]
        rows_in = [sem(f"rows_in{i}") for i in range(NT // 8)]
        y_in = [sem(f"y_in{i}") for i in range(4)]

        block = ctx.enter_context(nc.Block())
        NW, NB = 7, 8
        XQ = NJ // 4

        at = {}

        @block.gpsimd
        def _(po):
            n = [0]

            def made(name, ins):
                ins.then_inc(S["consts"], 1)
                n[0] += 1
                at[name] = n[0]
                po.wait_ge(S["consts"], n[0])

            def select(name, t, op, basev, pattern, cm, fill_value):
                made(name, po.affine_select(out=t, in_=t, compare_op=op, fill=fill_value, base=basev, pattern=pattern,
                                            channel_multiplier=cm))

            imp = dict(allow_small_or_imprecise_dtypes=True)
            made("id16", po.memset(id16[:, :], 0.0))
            select("id16", id16[:, :], ALU.not_equal, 0, [[-1, P]], 1, 1.0)
            made("fill", po.memset(fill, 0.0))
            made("fill", po.iota(fill[:, :, 2 * C:2 * C + 2].bitcast(I32), [[P, 4]], base=PAIRS, channel_multiplier=1))
            made("xs", po.memset(xs[:, :, 2 * C:], 0.0))
            made("xs", po.iota(xs[:, :, 2 * C:2 * C + 2].bitcast(I32), [[P, NJ]], base=0, channel_multiplier=1))
            made("blk", po.memset(blk[:, :, :], 1.0))
            select("blk", blk[:, :, :], ALU.is_ge, 0, [[-HD, HEADS], [0, HD]], 1, 0.0)
            select("blk", blk[:, :, :], ALU.is_ge, HD - 1, [[HD, HEADS], [0, HD]], -1, 0.0)
            with po.Fori(0, NG) as g:
                po.wait_ge(S["hi_ready"], g + 1)
                po.tensor_tensor(xs[:, ds(g * GT, GT), C:2 * C], xn[:, ds(g % (NG // 2), 1), :, :].rearrange("p a j c -> p (a j) c"),
                                 xs[:, ds(g * GT, GT), 0:C], ALU.subtract).then_inc(S["lo_ready"], 1)
            made("rank8", po.iota(rank8[:, :], [[-1, E]], base=E, channel_multiplier=0, **imp))
            made("before", po.memset(before[:, :], 1.0))
            select("before", before[:, :], ALU.is_ge, -1, [[1, P]], -1, 0.0)
            made("onesb", po.memset(onesb[:, :], 1.0))
            made("ones_row", po.memset(ones_row[:, :], 1.0))
            made("iota_t", po.iota(iota_t[:, :], [[1, NT + 4]], base=-2, channel_multiplier=0, **imp))
            made("kb_rows", po.memset(kb_rows[:, :], 0.0))
            made("b_rows", po.memset(b1_rows, 0.0))
            made("b_rows", po.memset(b2_rows, 0.0))
            made("ones16", po.memset(ones16[:, :], 1.0))
            made("chunk_of", po.memset(chunk_of[:, :, :], 0.0))
            select("chunk_of", chunk_of[:, :, :], ALU.not_equal, 0, [[-1, FC], [0, P]], 1, 1.0)
            select("chunk_of", chunk_of[:, :, :], ALU.not_equal, -32, [[-1, FC], [0, P]], 1, 1.0)
            made("t_const", po.iota(t_const[:, :], [[0, NJ]], base=T, channel_multiplier=0))
            po.wait_ge(S["biases_in"], 16 * NB)
            with po.Fori(0, NG) as g:
                po.tensor_tensor(xin[:, ds(g * GT, GT), :], xin[:, ds(g * GT, GT), :],
                                 bo_bc[:, :].unsqueeze(1).to_broadcast([P, GT, C]), ALU.add).then_inc(S["xb_ready"], 1)
            po.wait_ge(S["filled"], 64)
            po.wait_ge(S["slots_known"], 1)
            for i in range(2 * NJ):
                k, j = i // NJ, i % NJ
                if i >= 4:
                    po.wait_ge(place_in[i % 4], i // 4 * 16)
                if k and j % 8 == 0:
                    ids = xs[:, j:j + 8, 2 * C:2 * C + 2].bitcast(I32).rearrange("p j a -> p (j a)")
                    if j == 24:
                        for u in range(4):
                            po.wait_ge(place_in[u], 16 * (NJ // 4))
                    made("second", po.tensor_tensor(ids, ids, t_const[:, 0:8], ALU.add))
                po.indirect_dma_start(out=slot_dram, out_offset=bass.IndirectOffsetOnAxis(ap=slot_i[:, i:i + 1], axis=0),
                                      in_=xs[:, j, :], in_offset=None).then_inc(place_in[i % 4], 16)
            for t in range(NT):
                if t >= 4:
                    po.wait_ge(scatter_in[t % 4], t // 4 * 16)
                    po.sem_inc(S["y_free"], 1)
                po.wait_ge(S["y_out"], t + 1)
                po.indirect_dma_start(out=y_dram, out_offset=bass.IndirectOffsetOnAxis(ap=xg[:, t, 2 * C:2 * C + 2].bitcast(I32), axis=0),
                                      in_=yb[:, t % 4, :], in_offset=None).then_inc(scatter_in[t % 4], 16)

        @block.sync
        def _(sp):
            for i in range(4):
                sp.dma_start(xin[:, i * XQ:(i + 1) * XQ, :],
                             x_rows[i * XQ * P:(i + 1) * XQ * P].rearrange("(j p) c -> p j c", p=P)).then_inc(x_in[i], 16)
            for dst, src in ((bqk[:, 0:1], bq), (bqk[:, 1:2], bk), (bv_bc[:, :], bv.partition_broadcast(P)),
                             (bo_bc[:, :], bo.partition_broadcast(P)), (b1_raw[0:4, :, :], b1), (b1_raw[32:36, :, :], b1),
                             (b2_raw[0:1, :, :], b2), (b2_raw[32:33, :, :], b2)):
                sp.dma_start(dst, src).then_inc(S["biases_in"], 16)
            for i in range(4):
                sp.wait_ge(x_in[i], 16)
                sp.sem_inc(S["x_landed"], NG // 4)
            sp.dma_start(wraw[:, :], w1T).then_inc(S["w1_in"], 16)
            sp.dma_start(wraw2[:, :], w2T).then_inc(S["w2_in"], 16)
            sp.wait_ge(S["consts"], at["fill"])
            slots_v = slot_dram.rearrange("(r u p) c -> u p r c", u=4, p=P)
            for u in range(4):
                sp.dma_start(slots_v[u], fill[:, u, :].unsqueeze(1).to_broadcast([P, NT // 4, RW])).then_inc(S["filled"], 16)
            for u in range(4):
                sp.wait_ge(place_in[u], 16 * (2 * NJ // 4))
            sp.wait_ge(S["biases_split"], 1)
            for i in range(NT // 8):
                sp.dma_start(xg[:, i * 8:(i + 1) * 8, :],
                             slot_dram[i * 8 * P:(i + 1) * 8 * P].rearrange("(t p) c -> p t c", p=P)).then_inc(rows_in[i], 16)
            for i in range(NT // 8):
                sp.wait_ge(rows_in[i], 16)
                sp.sem_inc(S["rows_landed"], 8)
            for i in range(4):
                sp.wait_ge(scatter_in[i], 16 * (NT // 4))
            sp.wait_ge(S["w_lo"], 2 * NG)
            for i in range(4):
                for k, dst in ((0, wraw), (1, wraw2)):
                    rows = y_dram[k * T + i * XQ * P:k * T + (i + 1) * XQ * P]
                    sp.dma_start(dst[:, i * XQ * C:(i + 1) * XQ * C].rearrange("p (j c) -> p j c", c=C),
                                 rows.rearrange("(j p) c -> p j c", p=P)).then_inc(y_in[i], 16)
            for i in range(4):
                sp.wait_ge(S["summed"], (i + 1) * XQ)
                sp.dma_start(out_rows[i * XQ * P:(i + 1) * XQ * P].rearrange("(j p) c -> p j c", p=P),
                             xin[:, i * XQ:(i + 1) * XQ, :]).then_inc(S["stored"], 16)
            sp.wait_ge(S["stored"], 64)

        @block.scalar
        def _(ac):
            ac.dma_start(rw_raw[:, :], rwT).then_inc(S["rw_in"], 16)
            for dst, src in ((r_rep[:, :], R), (wnat[:, 0, :], wq), (wnat[:, 1, :], wk), (w3[:, 0, :], wqT),
                             (w3[:, 1, :], wkT), (w3[:, 2, :], wvT), (wo_sb[:, :], woT)):
                ac.dma_start(dst, src).then_inc(S["wsmall_in"], 16)

            def deviation(h):
                ac.wait_ge(S["stats"], h + 1)
                ac.activation(sd[:, :], veps[:, :], ACT.Sqrt).then_inc(S["sd_ready"], 1)

            def high(g):
                ac.wait_ge(S["xn_ready"], g + 1)
                b = g % (NG // 2)
                ac.activation(xs[:, ds(g * GT, GT), 0:C], xn[:, ds(b, 1), :, :].rearrange("p a j c -> p (a j) c"),
                              ACT.Copy).then_inc(S["hi_ready"], 1)

            def transposed(g, b):
                ac.wait_ge(S["xT_tr"], g + 1)
                ac.activation(xT[:, :, ds(g * GN, GN)],
                              bank[b][:, :].bitcast(F16).rearrange("p (s n) -> p s n", s=2), ACT.Copy).then_inc(S["xT_ready"], 1)

            def two_groups(g):
                high(g)
                transposed(g - 2, 0)
                high(g + 1)
                transposed(g - 1, 1)

            deviation(0)
            high(0)
            high(1)
            two_groups(2)
            deviation(1)
            with ac.Fori(NG // 4, NG // 2) as r:
                two_groups(r * 2)
            transposed(NG - 2, 0)
            transposed(NG - 1, 1)
            ac.wait_ge(S["w1_in"], 16)
            by_expert = "p (e n) -> p e n"
            ac.activation(w1h, wraw[:, :].rearrange(by_expert, e=E), ACT.Copy, scale=WS).then_inc(S["w_hi"], 1)
            ac.wait_ge(S["w2_in"], 16)
            ac.activation(w2h, wraw2[:, :].rearrange(by_expert, e=E), ACT.Copy, scale=WS).then_inc(S["w_hi"], 1)

            def square(ready, g, dst, b, done):
                ac.wait_ge(ready, g + 1)
                ac.activation(dst, bank[0][:, :], ACT.Square, scale=1.0 / WS, bias=bqk[:, b:b + 1]).then_inc(done, 1)

            def features(g):
                ac.wait_ge(S["q_expo"], g + 1)
                ac.activation(qf[:, :], bank[1][:, :], ACT.Exp, scale=1.0 / WS, bias=bpq[:, 0:1]).then_inc(S["q_feat"], 1)
                ac.wait_ge(S["k_expo"], g + 1)
                ac.activation(kf[:, :, :].rearrange("p j c -> p (j c)"), bank[2][:, :], ACT.Exp, scale=1.0 / WS).then_inc(S["k_feat"], 1)

            def squares(g):
                square(S["q_proj"], g, q2[:, :], 0, S["q_sq"])
                square(S["k_proj"], g, k2[:, :], 1, S["k_sq"])

            ac.wait_ge(S["bpq_ready"], 1)
            squares(0)
            with ac.Fori(0, NG - 1) as g:
                features(g)
                squares(g + 1)
            features(NG - 1)
            ac.wait_ge(S["exp_in"], 2)
            ac.activation(ex[:, :, :], dlt[:, :, :], ACT.Exp, scale=1.0 / RS).then_inc(S["exp_out"], 1)
            ac.activation(ex2[:, :], d2[:, :], ACT.Exp, scale=1.0 / RS).then_inc(S["exp_out"], 1)

            def rows(t, b):
                ac.wait_ge(S["slots_tr"], t + 1)
                ac.activation(xgT[:, b, :, :].rearrange("p s c -> p (s c)"), bank[b][:, 0:P].bitcast(F16), ACT.Copy).then_inc(S["slots_ready"], 1)

            def hidden(t, b):
                ac.wait_ge(S["h_ready"], t + 1)
                ac.activation(hh[:, b, :], bank[2 + b][:, :], ACT.Relu).then_inc(S["hh_ready"], 1)

            def output(t, u, wait_free=True):
                ac.wait_ge(S["y_ready"], t + 1)
                if wait_free:
                    ac.wait_ge(S["y_free"], t - 3)
                ac.activation(yb[:, u, :], bank[4 + u % 2][:, 0:C], ACT.Copy, scale=1.0 / (WS * WS)).then_inc(S["y_out"], 1)

            rows(0, 0)
            rows(1, 1)
            hidden(0, 0)
            for t in range(4):
                rows(t + 2, t % 2)
                hidden(t + 1, (t + 1) % 2)
                output(t, t, wait_free=False)
            with ac.Fori(1, NT // 4 - 1) as r:
                for u in range(4):
                    rows(r * 4 + u + 2, u % 2)
                    hidden(r * 4 + u + 1, (u + 1) % 2)
                    output(r * 4 + u, u)
            for t in range(NT - 4, NT):
                if t + 2 < NT:
                    rows(t + 2, t % 2)
                if t + 1 < NT:
                    hidden(t + 1, (t + 1) % 2)
                output(t, t % 4)

        @block.vector
        def _(ve):
            n = [0]

            def step(ins):
                ins.then_inc(S["dve"], 1)
                n[0] += 1
                ve.wait_ge(S["dve"], n[0])

            ve.wait_ge(S["rw_in"], 16)
            step(ve.tensor_scalar(rw[:, 0, :], rw_raw[:, :], RS, None, ALU.mult))
            ve.scalar_tensor_tensor(rw[:, 1, :], rw_raw[:, :], RS, rw[:, 0, :], ALU.mult, ALU.subtract).then_inc(S["rw_ready"], 1)
            HG = NG // 2
            for h in range(2):
                with ve.Fori(h * HG, (h + 1) * HG) as g:
                    ve.wait_ge(S["x_landed"], g + 1)
                    for j in range(GT):
                        ve.bn_stats(st6[:, ds((g - h * HG) * GT + j, 1), :].rearrange("p a c -> p (a c)"),
                                    xin[:, ds(g * GT + j, 1), :].rearrange("p a c -> p (a c)"))
                ve.drain()
                for i in range(HJ):
                    ve.bn_aggr(mv[:, i, :], st6[:, i, :])
                ve.drain()
                step(ve.tensor_scalar(veps[:, :], mv[:, :, 1], 1e-5, None, ALU.add))
                ve.sem_inc(S["stats"], 1)
                ve.wait_ge(S["sd_ready"], h + 1)
                step(ve.reciprocal(rs0[:, :], sd[:, :]))
                step(ve.tensor_tensor(rs1[:, :], rs0[:, :], rs0[:, :], ALU.mult))
                step(ve.tensor_tensor(rs2[:, :], rs1[:, :], veps[:, :], ALU.mult))
                step(ve.tensor_scalar(rs1[:, :], rs2[:, :], -0.5, 1.5, ALU.mult, ALU.add))
                step(ve.tensor_tensor(rstd[:, :], rs0[:, :], rs1[:, :], ALU.mult))
                with ve.Fori(h * HG, (h + 1) * HG) as g:
                    if h:
                        ve.wait_ge(S["lo_ready"], g - HG + 1)
                    for j in range(GT):
                        i = (g - h * HG) * GT + j
                        last = ve.tensor_scalar(xn[:, ds(g - h * HG, 1), j, :].rearrange("p a c -> p (a c)"),
                                                xin[:, ds(g * GT + j, 1), :].rearrange("p a c -> p (a c)"),
                                                mv[:, ds(i, 1), 0:1].rearrange("p a c -> p (a c)"), rstd[:, ds(i, 1)],
                                                ALU.subtract, ALU.mult)
                    last.then_inc(S["xn_ready"], 1)

            ve.wait_ge(S["consts"], at["blk"])
            ve.wait_ge(S["wsmall_in"], 16 * NW)
            ve.wait_ge(S["biases_in"], 16 * NB)
            ve.tensor_copy(bk_wide[:, :], bqk[:, 1:2].to_broadcast([P, C]))
            ve.scalar_tensor_tensor(rblk[:, :].rearrange("p (h d) -> p h d", d=HD),
                                    r_rep[:, :].unsqueeze(1).to_broadcast([P, HEADS, HD]), WS / HD ** 0.5, blk[:, :, :],
                                    ALU.mult, ALU.mult).then_inc(S["rblk_ready"], 1)
            ve.tensor_scalar(negblk[:, :], blk[:, :, :].rearrange("p h d -> p (h d)"), -1.0, None, ALU.mult)
            ve.tensor_scalar(bv_bc[:, :], bv_bc[:, :], WS, None, ALU.mult)
            step(ve.tensor_scalar(WH[:, 0:3, :], w3[:, :, :], WS, None, ALU.mult))
            step(ve.scalar_tensor_tensor(WL[:, 0:3, :], w3[:, :, :], WS, WH[:, 0:3, :], ALU.mult, ALU.subtract))

            def over_e(a):
                return a.unsqueeze(2).to_broadcast([P, NJ, E])

            def first_max(src, m, pick):
                step(ve.tensor_reduce(m[:, :], src[:, :, :], AX.X, ALU.max))
                step(ve.tensor_tensor(eq[:, :, :], src[:, :, :], over_e(m[:, :]), ALU.is_equal))
                step(ve.tensor_tensor(sc[:, :, :], eq[:, :, :], rank8[:, :].unsqueeze(1).to_broadcast([P, NJ, E]), ALU.mult))
                step(ve.tensor_reduce(mx[:, :], sc[:, :, :], AX.X, ALU.max))
                step(ve.tensor_tensor(pick[:, :, :], sc[:, :, :], over_e(mx[:, :]), ALU.is_equal))

            ve.wait_ge(S["consts"], at["b_rows"])
            ve.wait_ge(S["logits"], 1)
            step(ve.tensor_copy(lg[:, :, :].rearrange("p j e -> p (j e)"), bank[7][:, 0:NJ * E]))
            first_max(lg, m1, pick1)
            step(ve.scalar_tensor_tensor(lg2[:, :, :], pick1[:, :, :], -1e30, lg[:, :, :], ALU.mult, ALU.add))
            first_max(lg2, m2, pick2)
            ve.tensor_tensor(took[:, :, :].rearrange("p e j -> p j e"), pick1[:, :, :], pick2[:, :, :], ALU.add).then_inc(S["took_ready"], 1)
            ve.wait_ge(S["folded"], 1)
            step(ve.tensor_copy(WH[:, 3:5, :].rearrange("p a c -> p (a c)"), bank[0][:, 0:2 * C]))
            step(ve.tensor_tensor(WL[:, 3:5, :].rearrange("p a c -> p (a c)"), bank[0][:, 0:2 * C],
                                  WH[:, 3:5, :].rearrange("p a c -> p (a c)"), ALU.subtract))
            step(ve.tensor_copy(kb_hi[:, :], bank[1][:, 0:C]))
            ve.tensor_copy(kb_rows[0:1, :], kb_hi[0:1, :])
            ve.tensor_tensor(kb_rows[32:33, :], bank[1][32:33, 0:C], kb_hi[32:33, :], ALU.subtract)
            ve.tensor_scalar(bpq[:, :], bank[1][:, C:C + 1], 1.0 / WS, None, ALU.mult).then_inc(S["bpq_ready"], 1)
            ve.wait_ge(S["counts"], 1)
            step(ve.tensor_copy(tot[:, :, :].rearrange("p e j -> p (e j)"), bank[6][:, 0:E * NJ]))
            step(ve.tensor_tensor_scan(run[:, :, :].rearrange("p e j -> p (e j)"), ones_row[:, :],
                                       tot[:, :, :].rearrange("p e j -> p (e j)"), 0.0, ALU.mult, ALU.add))
            ve.tensor_tensor(exc[:, :, :], run[:, :, :], tot[:, :, :], ALU.subtract)
            step(ve.tensor_reduce(cnt[:, :], tot[:, :, :], AX.X, ALU.add))
            step(ve.tensor_scalar(cnt_i[:, :], cnt[:, :], float(P - 1), None, ALU.add))
            step(ve.tensor_scalar(nt_i[:, :], cnt_i[:, :], 7, None, ALU.arith_shift_right))
            step(ve.tensor_copy(nt_f[:, :], nt_i[:, :]))
            step(ve.tensor_tensor_scan(end_t[:, :], ones_row[:, 0:E], nt_f[:, :], 0.0, ALU.mult, ALU.add))
            step(ve.tensor_tensor(base[:, :], end_t[:, :], nt_f[:, :], ALU.subtract))
            step(ve.scalar_tensor_tensor(offs[:, :], base[:, :], float(P), exc[:, :, 0], ALU.mult, ALU.subtract))
            step(ve.tensor_tensor(pos[:, :, :].rearrange("p e j -> p (e j)"), bank[5][:, 0:E * NJ],
                                  exc[:, :, :].rearrange("p e j -> p (e j)"), ALU.add))
            step(ve.tensor_tensor(pos2[:, :, :], pos[:, :, :], offs[:, :].unsqueeze(2).to_broadcast([P, E, NJ]), ALU.add))
            for k, pick in enumerate((pick1, pick2)):
                step(ve.tensor_tensor(ppick[:, :, :], pick[:, :, :], pos2[:, :, :].rearrange("p e j -> p j e"), ALU.mult))
                step(ve.tensor_reduce(slot[:, k * NJ:(k + 1) * NJ], ppick[:, :, :], AX.X, ALU.add))
            ve.tensor_copy(slot_i[:, :], slot[:, :]).then_inc(S["slots_known"], 1)

            def values(g):
                ve.wait_ge(S["v_proj"], g + 1)
                ve.tensor_tensor(vv[:, :, :], bank[3][:, :].rearrange("p (j c) -> p j c", j=GT),
                                 bv_bc[:, :].unsqueeze(1).to_broadcast([P, GT, C]), ALU.add).then_inc(S["v_ready"], 1)

            def residual(g):
                ve.wait_ge(S["wo_out"], g + 1)
                ve.tensor_tensor(xin[:, ds(g * GT, GT), :], bank[7][:, :].rearrange("p (j c) -> p j c", j=GT),
                                 xin[:, ds(g * GT, GT), :], ALU.add).then_inc(S["acc_ready"], 1)

            def weights_low(g):
                for i, raw in ((0, wraw), (2, wraw2)):
                    hi, lo = (wsets[:, ds(g * WSET + (i + s) * F, F)] for s in range(2))
                    ve.scalar_tensor_tensor(lo, raw[:, ds(g * F, F)], WS, hi, ALU.mult, ALU.subtract).then_inc(S["w_lo"], 1)

            def weigh(g):
                ve.wait_ge(S["dens"], g + 1)
                ve.tensor_scalar(zz[:, :], bank[6][:, :], 1e-8, None, ALU.add).then_inc(S["dens_read"], 1)
                ve.drain()
                ve.reciprocal(rz[:, :], zz[:, :])
                ve.wait_ge(S["kv_sum"], g + 1)
                ve.scalar_tensor_tensor(kvm[:, :, :], bank[4][:, 0:2 * C].rearrange("p (b c) -> p b c", b=2), 1.0 / WS,
                                        blk[:, :, :].rearrange("p h d -> p (h d)").unsqueeze(1).to_broadcast([P, 2, C]),
                                        ALU.mult, ALU.mult).then_inc(S["kv_ready"], 1)
                ve.wait_ge(S["nums"], g + 1)
                ve.tensor_tensor(oT[:, :], bank[5][:, :], rz[:, :], ALU.mult).then_inc(S["oT_ready"], 1)

            def dve_group(g, first=False):
                values(g)
                if not first:
                    residual(g - 1)
                weights_low(g)
                weigh(g)

            ve.wait_ge(S["w_hi"], 2)
            ve.wait_ge(S["xb_ready"], NG)
            dve_group(0, first=True)
            for rows, raw, hi, n0, scale in ((b1_rows, b1_raw, b1_hi, FC, WS), (b2_rows, b2_raw, b2_hi, 1, WS * WS)):
                ve.tensor_scalar(rows[0:n0, :, :], raw[0:n0, :, :], scale, None, ALU.mult)
                step(ve.tensor_scalar(hi[32:32 + n0, :, :], raw[32:32 + n0, :, :], scale, None, ALU.mult))
                step(ve.scalar_tensor_tensor(rows[32:32 + n0, :, :], raw[32:32 + n0, :, :], scale,
                                             hi[32:32 + n0, :, :], ALU.mult, ALU.subtract))
            ve.sem_inc(S["biases_split"], 1)
            step(ve.tensor_tensor(cmp_t[:, :, :], end_t[:, :].unsqueeze(1).to_broadcast([P, NT + 4, E]),
                                  iota_t[:, :].unsqueeze(2).to_broadcast([P, NT + 4, E]), ALU.is_le))
            step(ve.tensor_reduce(et_f[:, :], cmp_t[:, :, :], AX.X, ALU.add))
            ve.tensor_scalar(et_i[:, :], et_f[:, :], float(E - 1), float(WSET), ALU.min, ALU.mult).then_inc(S["experts_known"], 1)
            ve.tensor_tensor(dlt[:, :, :], lg[:, :, :], over_e(m1[:, :]), ALU.subtract).then_inc(S["exp_in"], 1)
            ve.tensor_tensor(d2[:, :], m2[:, :], m1[:, :], ALU.subtract).then_inc(S["exp_in"], 1)
            with ve.Fori(1, NG) as g:
                dve_group(g)
            residual(NG - 1)

            regs = [ctx.enter_context(ve.register(f"set{i}")) for i in range(4)]

            def load_experts(r):
                ve.reg_load(regs, et_i[0:1, ds(r * 4, 4)])
                return [ve.snap(x, min_val=0, max_val=(E - 1) * WSET) for x in regs]

            def fetch_set(t, u, e, wait_used=True):
                if wait_used:
                    ve.wait_ge(S["y_ready"], t - 3)
                ve.tensor_copy(wset[u], wsets[:, ds(e, WSET)]).then_inc(S["set_ready"], 1)

            def low(t, b):
                ve.wait_ge(S["hh_ready"], t + 1)
                ve.scalar_tensor_tensor(hl[:, b, :], bank[2 + b][:, :], 0.0, hh[:, b, :], ALU.max, ALU.subtract).then_inc(S["hl_ready"], 1)

            def four_tiles(r, first=False):
                e = load_experts(r + 1)
                for u in range(4):
                    t = r * 4 + u
                    fetch_set(t + 2, (u + 2) % 4, e[u], wait_used=not (first and u < 2))
                    low(t + 1, (u + 1) % 2)

            ve.wait_ge(S["rows_landed"], 8)
            ve.wait_ge(S["experts_known"], 1)
            e = load_experts(0)
            fetch_set(0, 0, e[2], wait_used=False)
            fetch_set(1, 1, e[3], wait_used=False)
            low(0, 0)
            four_tiles(0, first=True)
            with ve.Fori(1, NT // 4 - 1) as r:
                four_tiles(r)
            e = load_experts(NT // 4)
            fetch_set(NT - 2, 2, e[0])
            low(NT - 3, 1)
            fetch_set(NT - 1, 3, e[1])
            low(NT - 2, 0)
            low(NT - 1, 1)

            ve.wait_ge(S["exp_out"], 2)
            step(ve.tensor_reduce(ssum[:, :], ex[:, :, :], AX.X, ALU.add))
            step(ve.reciprocal(pr1[:, :], ssum[:, :]))
            step(ve.tensor_tensor(pr2[:, :], ex2[:, :], pr1[:, :], ALU.mult))
            step(ve.scalar_tensor_tensor(den[:, :], pr2[:, :], 1e-9, pr1[:, :], ALU.add, ALU.add))
            step(ve.reciprocal(rden[:, :], den[:, :]))
            ve.tensor_tensor(gate1[:, :], pr1[:, :], rden[:, :], ALU.mult)
            step(ve.tensor_tensor(gate2[:, :], pr2[:, :], rden[:, :], ALU.mult))
            for i in range(4):
                ve.wait_ge(y_in[i], 32)
                for k, (y, gate) in enumerate(((wraw, gate1), (wraw2, gate2))):
                    with ve.Fori(i * XQ // 4, (i + 1) * XQ // 4) as r:
                        for u in range(4):
                            j = r * 4 + u
                            acc = xin[:, ds(j, 1), :].rearrange("p a c -> p (a c)")
                            last = ve.scalar_tensor_tensor(acc, y[:, ds(j * C, C)], gate[:, ds(j, 1)], acc, ALU.mult, ALU.add)
                        if k == 1:
                            last.then_inc(S["summed"], 4)
                    if k == 0:
                        ve.drain()

        @block.tensor
        def _(pe):
            def mm(o, l, r, start=False, stop=False):
                return pe.matmul(o, l, r, start=start, stop=stop, skip_group_check=True)

            def transposes(g, b, first=False):
                pe.wait_ge(S["hi_ready"], g + 1)
                pe.wait_ge(S["lo_ready"], g + 1)
                if not first:
                    pe.wait_ge(S["xT_ready"], g - 1)
                o = bank[b][:, :].bitcast(F16)
                for s in range(2):
                    for j in range(GT):
                        to = (s * GT + j) * P
                        last = pe.transpose(o[:, to:to + P],
                                            xs[:, ds(g * GT + j, 1), s * C:(s + 1) * C].rearrange("p a c -> p (a c)"), id16[:, :])
                last.then_inc(S["xT_tr"], 1)

            def router(g):
                pe.wait_ge(S["xT_ready"], g + 1)
                for j in range(GT):
                    o = bank[7][:, ds((g * GT + j) * E, E)]
                    hi = xT[:, 0, ds(g * GN + j * P, P)]
                    mm(o, hi, rw[:, 0, :], start=isinstance(g, int) and g == 0 and j == 0)
                    mm(o, hi, rw[:, 1, :])
                    last = mm(o, xT[:, 1, ds(g * GN + j * P, P)], rw[:, 0, :], stop=True)
                return last

            pe.wait_ge(S["consts"], at["id16"])
            transposes(0, 0, first=True)
            transposes(1, 1, first=True)
            pe.wait_ge(S["rw_ready"], 1)
            router(0)
            with pe.Fori(1, NG // 2) as r:
                transposes(r * 2, 0)
                router(r * 2 - 1)
                transposes(r * 2 + 1, 1)
                router(r * 2)
            router(NG - 1).then_inc(S["logits"], 1)
            pe.wait_ge(S["rblk_ready"], 1)
            mm(bank[0][:, 0:C], wnat[:, 0, :], rblk[:, :], start=True, stop=True)
            mm(bank[0][:, C:2 * C], wnat[:, 1, :], rblk[:, :], start=False, stop=True)
            mm(bank[1][:, 0:C], bk_wide[:, :], rblk[:, :], start=True, stop=True)
            mm(bank[1][:, C:C + 1], rblk[:, :], bqk[:, 0:1], start=False, stop=True).then_inc(S["folded"], 1)
            pe.wait_ge(S["consts"], at["b_rows"])
            pe.wait_ge(S["took_ready"], 1)
            flat = took[:, :, :].rearrange("p e j -> p (e j)")
            mm(bank[5][:, 0:E * NJ], before[:, :], flat, start=True, stop=True)
            mm(bank[6][:, 0:E * NJ], onesb[:, :], flat, start=True, stop=True).then_inc(S["counts"], 1)

            def project(g, w):
                for n_, (a, b) in enumerate(((WH, 0), (WH, 1), (WL, 0))):
                    m = mm(bank[0][:, :], a[:, w, :], xT[:, b, ds(g * GN, GN)], start=(n_ == 0), stop=(n_ == 2))
                return m

            def project_q(g, first=False):
                if not first:
                    pe.wait_ge(S["k_sq"], g)
                project(g, Q).then_inc(S["q_proj"], 1)

            def project_k(g):
                pe.wait_ge(S["q_sq"], g + 1)
                project(g, K).then_inc(S["k_proj"], 1)

            def exponents_a(g, first=False):
                if not first:
                    pe.wait_ge(S["q_feat"], g)
                for n_, (a, b) in enumerate(((WH, 0), (WH, 1), (WL, 0))):
                    mm(bank[1][:, :], a[:, PQ, :], xT[:, b, ds(g * GN, GN)], start=(n_ == 0))
                if not first:
                    pe.wait_ge(S["k_feat"], g)
                for j in range(GT):
                    o = bank[2][:, j * P:(j + 1) * P]
                    hi, lo = (xT[:, b, ds(g * GN + j * P, P)] for b in range(2))
                    mm(o, hi, WH[:, PK, :], start=(j == 0))
                    mm(o, hi, WL[:, PK, :])
                    mm(o, lo, WH[:, PK, :])
                    mm(o, ones16[:, :], kb_rows[:, :])
                if not first:
                    pe.wait_ge(S["v_ready"], g)
                for j in range(GT):
                    o = bank[3][:, j * P:(j + 1) * P]
                    hi, lo = (xT[:, b, ds(g * GN + j * P, P)] for b in range(2))
                    mm(o, hi, WH[:, V, :], start=(j == 0))
                    mm(o, hi, WL[:, V, :])
                    m = mm(o, lo, WH[:, V, :], stop=True)
                m.then_inc(S["v_proj"], 1)

            def exponents_b(g):
                pe.wait_ge(S["q_sq"], g + 1)
                mm(bank[1][:, :], negblk[:, :], q2[:, :], stop=True).then_inc(S["q_expo"], 1)
                pe.wait_ge(S["k_sq"], g + 1)
                for j in range(GT):
                    m = mm(bank[2][:, j * P:(j + 1) * P], k2[:, j * P:(j + 1) * P], negblk[:, :], stop=True)
                m.then_inc(S["k_expo"], 1)

            def sums(g, first=False):
                pe.wait_ge(S["k_feat"], g + 1)
                pe.wait_ge(S["v_ready"], g + 1)
                if not first:
                    pe.wait_ge(S["kv_ready"], g)
                for b in range(2):
                    for s in range(2):
                        m = mm(bank[4][:, b * C:(b + 1) * C], kf[:, 2 * b + s, :], vv[:, 2 * b + s, :],
                               start=(b == 0 and s == 0), stop=(s == 1))
                m.then_inc(S["kv_sum"], 1)

            def denominators(g, first=False):
                pe.wait_ge(S["q_feat"], g + 1)
                if not first:
                    pe.wait_ge(S["dens_read"], g)
                mm(bank[6][:, :], blk[:, :, :].rearrange("p h d -> p (h d)"), qf[:, :], start=True, stop=True).then_inc(S["dens"], 1)

            def numerators(g, first=False):
                pe.wait_ge(S["kv_ready"], g + 1)
                if not first:
                    pe.wait_ge(S["oT_ready"], g)
                for b in range(2):
                    m = mm(bank[5][:, b * 2 * P:(b + 1) * 2 * P], kvm[:, b, :], qf[:, b * 2 * P:(b + 1) * 2 * P],
                           start=(b == 0), stop=True)
                m.then_inc(S["nums"], 1)

            def project_out(g, first=False):
                pe.wait_ge(S["oT_ready"], g + 1)
                if not first:
                    pe.wait_ge(S["acc_ready"], g)
                for a in range(GT):
                    m = mm(bank[7][:, a * P:(a + 1) * P], oT[:, a * P:(a + 1) * P], wo_sb[:, :], start=(a == 0), stop=True)
                m.then_inc(S["wo_out"], 1)

            def pe_group(g, first=False, last=False, out_first=False):
                exponents_a(g, first)
                exponents_b(g)
                if not first:
                    project_out(g - 1, out_first)
                if not last:
                    project_q(g + 1)
                denominators(g, first)
                if not last:
                    project_k(g + 1)
                sums(g, first)
                numerators(g, first)

            pe.wait_ge(S["consts"], at["ones16"])
            pe.wait_ge(S["bpq_ready"], 1)
            project_q(0, first=True)
            project_k(0)
            pe.wait_ge(S["slots_known"], 1)
            pe_group(0, first=True)
            pe_group(1, out_first=True)
            with pe.Fori(2, NG - 1) as g:
                pe_group(g)
            pe_group(NG - 1, last=True)
            project_out(NG - 1)

            def slots(t, b, first=False):
                pe.wait_ge(S["rows_landed"], t + 1)
                if not first:
                    pe.wait_ge(S["slots_ready"], t - 1)
                o = bank[b][:, 0:P].bitcast(F16)
                for s in range(2):
                    m = pe.transpose(o[:, s * P:(s + 1) * P], xg[:, ds(t, 1), s * C:(s + 1) * C].rearrange("p a c -> p (a c)"), id16[:, :])
                m.then_inc(S["slots_tr"], 1)

            def layer1(t, u, first=False):
                b = u % 2
                pe.wait_ge(S["set_ready"], t + 1)
                pe.wait_ge(S["slots_ready"], t + 1)
                if not first:
                    pe.wait_ge(S["hl_ready"], t - 1)
                mm(bank[2 + b][:, :], wset[u][:, 4 * F:4 * F + P], chunk_of[:, :, :].rearrange("p f n -> p (f n)"), start=True)
                for c in range(FC):
                    o = bank[2 + b][:, c * P:(c + 1) * P]
                    h, l = (wset[u][:, s * F + c * P:s * F + (c + 1) * P] for s in range(2))
                    mm(o, h, xgT[:, b, 0, :])
                    mm(o, h, xgT[:, b, 1, :])
                    m = mm(o, l, xgT[:, b, 0, :], stop=(c == FC - 1))
                m.then_inc(S["h_ready"], 1)

            def layer2(t, u, first=False):
                b = u % 2
                w2h, w2l = (wset[u][:, s * F:(s + 1) * F] for s in (2, 3))
                if not first:
                    pe.wait_ge(S["y_out"], t - 1)
                o = bank[4 + b][:, 0:C]
                mm(o, ones16[:, :], wset[u][:, 4 * F + P:], start=True)
                pe.wait_ge(S["hh_ready"], t + 1)
                for c in range(FC):
                    mm(o, hh[:, b, c * P:(c + 1) * P], w2h[:, c * C:(c + 1) * C])
                    mm(o, hh[:, b, c * P:(c + 1) * P], w2l[:, c * C:(c + 1) * C])
                pe.wait_ge(S["hl_ready"], t + 1)
                for c in range(FC):
                    m = mm(o, hl[:, b, c * P:(c + 1) * P], w2h[:, c * C:(c + 1) * C], stop=(c == FC - 1))
                m.then_inc(S["y_ready"], 1)

            def four_tiles(r, first=False, last=False):
                for u in range(4):
                    t = r * 4 + u
                    if not (last and u >= 2):
                        slots(t + 2, u % 2)
                    if not (last and u == 3):
                        layer1(t + 1, (u + 1) % 4, first=(first and u == 0))
                    layer2(t, u, first=(first and u < 2))

            pe.wait_ge(S["consts"], at["chunk_of"])
            pe.wait_ge(S["acc_ready"], NG)
            slots(0, 0, first=True)
            slots(1, 1, first=True)
            layer1(0, 0, first=True)
            four_tiles(0, first=True)
            with pe.Fori(1, NT // 4 - 1) as r:
                four_tiles(r)
            four_tiles(NT // 4 - 1, last=True)


def kernel(L0_attn_x, L0_attn_Wq, L0_attn_bq, L0_attn_Wk, L0_attn_bk, L0_attn_Wv, L0_attn_bv, L0_attn_Wo, L0_attn_bo,
           L0_attn_R, L0_ffn_router_w, L0_ffn_w1, L0_ffn_b1, L0_ffn_w2, L0_ffn_b2):
    import numpy as np
    import concourse.bacc as bacc
    from concourse.bass_utils import run_bass_kernel_spmd

    a = np.asarray
    w1, w2 = a(L0_ffn_w1), a(L0_ffn_w2)
    arrays = {
        "x": a(L0_attn_x),
        "wq": a(L0_attn_Wq), "wk": a(L0_attn_Wk),
        "wqT": a(L0_attn_Wq).T, "wkT": a(L0_attn_Wk).T, "wvT": a(L0_attn_Wv).T, "woT": a(L0_attn_Wo).T,
        "bq": a(L0_attn_bq)[:, None], "bk": a(L0_attn_bk)[:, None], "bv": a(L0_attn_bv), "bo": a(L0_attn_bo),
        "R": np.tile(a(L0_attn_R), (HEADS, 1)),
        "rwT": a(L0_ffn_router_w).T,
        "w1T": w1.transpose(2, 0, 1).reshape(C, E * F),
        "b1": a(L0_ffn_b1).reshape(E, FC, P).transpose(1, 0, 2),
        "w2T": w2.reshape(E, C, FC, P).transpose(3, 0, 2, 1).reshape(P, E * FC * C),
        "b2": a(L0_ffn_b2)[None],
    }
    arrays = {f"in_{k}": np.ascontiguousarray(v) for k, v in arrays.items()}
    nc = bacc.Bacc("TRN2", target_bir_lowering=False, num_devices=1)
    args = [nc.dram_tensor(k, v.shape, mybir.dt.from_np(v.dtype), kind="ExternalInput").ap() for k, v in arrays.items()]
    result = nc.dram_tensor("out_0", (16, 256, 128), F32, kind="ExternalOutput").ap()
    build(nc, *args, result)
    r = run_bass_kernel_spmd(nc, [arrays], core_ids=[0])
    return r.results[0]["out_0"]
```

```python
from contextlib import ExitStack

import concourse.bass as bass
from concourse import mybir

F32 = mybir.dt.float32
F16 = mybir.dt.float16
BF16 = mybir.dt.bfloat16
I32 = mybir.dt.int32
I16 = mybir.dt.int16
ALU = mybir.AluOpType
ACT = mybir.ActivationFunctionType
AX = mybir.AxisListType
ds = bass.ds

P = 128
C = 128
HEADS, HD = 16, 8
E, F = 8, 512
FC = F // P
WS = 16.0
RS = 1024.0
Q, K, V, PQ, PK = range(5)


def build(nc, x, wq, wk, wqT, wkT, wvT, woT, bq, bk, bv, bo, R, rwT, w1T, b1, w2T, b2, out):
    T = x.shape[0] * x.shape[1]
    NJ = T // P
    GT = 4
    GN = GT * P
    NG = NJ // GT
    NT = 2 * T // P + E
    PAIRS = 2 * T
    assert NT % 4 == 0 and x.shape[1] == 2 * P

    x_rows = x.rearrange("b n c -> (b n) c")
    out_rows = out.rearrange("b n c -> (b n) c")
    RW = 2 * C + 8
    slot_dram = nc.dram_tensor("slot_dram", [NT * P, RW], F16).ap()
    y_dram = nc.dram_tensor("y_dram", [PAIRS + 4 * P, C], F32).ap()

    with ExitStack() as ctx:
        def sb(name, shape, dt=F32):
            return ctx.enter_context(nc.sbuf_tensor(name, shape, dt))

        def sem(name):
            return ctx.enter_context(nc.semaphore(name))

        bank = [ctx.enter_context(nc.psum_tensor(f"bank{i}", [P, 512], F32)) for i in range(8)]

        xin = sb("xin", [P, NJ, C])
        xs = sb("xs", [P, NJ, RW], F16)
        xT = sb("xT", [P, 2, T], F16)
        xg = sb("xg", [P, NT, RW], F16)
        WSET = 4 * F + C + 2 * FC
        wset_ints = sb("wsets", [P, E * WSET], I16)
        wsets = wset_ints[:, :].bitcast(F16)
        wv = wsets[:, :].rearrange("p (e n) -> p e n", e=E)
        w1h, w1l, w2h, w2l = (wv[:, :, i * F:(i + 1) * F] for i in range(4))
        b2_rows = wv[:, :, 4 * F:4 * F + C]
        b1_cols = wsets[:, :].bitcast(F32).rearrange("p (e n) -> p e n", e=E)[:, :, WSET // 2 - FC:]
        wraw = sb("wraw", [P, E * F])
        wraw2 = sb("wraw2", [P, E * F])
        early = xg[:, :, :].rearrange("p t c -> p (t c)")
        b1_raw = early[:, 0:2 * E * FC].bitcast(F32).rearrange("p (e f) -> p e f", e=E)
        b2_raw = early[:, 2048:4096].bitcast(F32).rearrange("p (e f) -> p e f", e=E)
        b2_hi = early[:, 5120:6144].rearrange("p (e f) -> p e f", e=E)
        fill = early[:, 6144:6144 + 4 * RW].rearrange("p (u c) -> p u c", u=4)
        wnat = sb("wnat", [P, 2, C])
        w3 = sb("w3", [P, 3, C])
        wo_sb = sb("wo_sb", [P, C])
        WH = sb("WH", [P, 5, C], F16)
        WL = sb("WL", [P, 5, C], F16)
        r_rep = sb("r_rep", [P, HD])
        rblk = sb("rblk", [P, C])
        rw_raw = sb("rw_raw", [P, E])
        rw = sb("rw", [P, 2, E], F16)
        bqk = sb("bqk", [P, 2])
        bk_wide = sb("bk_wide", [P, C])
        bpq = sb("bpq", [P, 1])
        bv_bc = sb("bv_bc", [P, C])
        bo_bc = sb("bo_bc", [P, C])
        kb_rows = sb("kb_rows", [P, C], F16)
        kb_hi = sb("kb_hi", [P, C], F16)
        id16 = sb("id16", [P, P], F16)
        id32 = sb("id32", [P, P])
        ones16 = sb("ones16", [P, P], F16)
        onesb = sb("onesb", [P, P], BF16)
        before = sb("before", [P, P], BF16)
        blk = sb("blk", [P, HEADS, HD])
        negblk = sb("negblk", [P, C])
        rank8 = sb("rank8", [P, E])
        iota_t = sb("iota_t", [P, NT + 4])
        t_const = sb("t_const", [P, NJ], I32)
        ones_row = sb("ones_row", [P, E * NJ])
        HJ = NJ // 2
        st6 = sb("st6", [P, HJ, 6])
        mv = sb("mv", [P, HJ, 2])
        veps = sb("veps", [P, HJ])
        sd = sb("sd", [P, HJ])
        rs0 = sb("rs0", [P, HJ])
        rs1 = sb("rs1", [P, HJ])
        rs2 = sb("rs2", [P, HJ])
        rstd = sb("rstd", [P, HJ])
        xn = sb("xn", [P, NG // 2, GT, C])
        lg = sb("lg", [P, NJ, E])
        m1 = sb("m1", [P, NJ])
        m2 = sb("m2", [P, NJ])
        eq = sb("eq", [P, NJ, E])
        sc = sb("sc", [P, NJ, E])
        mx = sb("mx", [P, NJ])
        pick1 = sb("pick1", [P, NJ, E])
        pick2 = sb("pick2", [P, NJ, E])
        lg2 = sb("lg2", [P, NJ, E])
        dlt = sb("dlt", [P, NJ, E])
        d2 = sb("d2", [P, NJ])
        ex = sb("ex", [P, NJ, E])
        ex2 = sb("ex2", [P, NJ])
        ssum = sb("ssum", [P, NJ])
        pr1 = sb("pr1", [P, NJ])
        pr2 = sb("pr2", [P, NJ])
        den = sb("den", [P, NJ])
        rden = sb("rden", [P, NJ])
        gate1 = sb("gate1", [P, NJ])
        gate2 = sb("gate2", [P, NJ])
        took = sb("took", [P, E, NJ], BF16)
        run = sb("run", [P, E, NJ])
        exc = sb("exc", [P, E, NJ])
        cnt = sb("cnt", [P, E])
        cnt_i = sb("cnt_i", [P, E], I32)
        nt_i = sb("nt_i", [P, E], I32)
        nt_f = sb("nt_f", [P, E])
        end_t = sb("end_t", [P, E])
        base = sb("base", [P, E])
        offs = sb("offs", [P, E])
        pos = sb("pos", [P, E, NJ])
        pos2 = sb("pos2", [P, E, NJ])
        ppick = sb("ppick", [P, NJ, E])
        slot = sb("slot", [P, 2 * NJ])
        slot_i = sb("slot_i", [P, 2 * NJ], I32)
        cmp_t = sb("cmp_t", [P, NT + 4, E])
        et_f = sb("et_f", [P, NT + 4])
        et_i = sb("et_i", [P, NT + 4], I32)
        q2, k2, qf, kf2 = (xn[:, i, :, :].rearrange("p j c -> p (j c)") for i in range(4))
        vv2, oo2, oT = (sb(f"att{i}", [P, GN]) for i in range(3))
        zz = sb("zz", [P, 2, 2, HEADS])
        zr = sb("zr", [P, 2, 2, HEADS])
        kf, vv, oo = (a.rearrange("p (j c) -> p j c", j=GT) for a in (kf2, vv2, oo2))
        NUM = C + HEADS
        kvm = sb("kvm", [P, 2, NUM])
        hidden_bank = [bank[i] for i in (2, 3, 6, 7)]
        free2 = xT[:, :, :].rearrange("p s n -> p (s n)")
        xgT = free2[:, 0:4 * P].rearrange("p (b s n) -> p b s n", b=2, s=2)
        hh = free2[:, 1024:1024 + 2 * F].rearrange("p (b f) -> p b f", b=2)
        hl = free2[:, 2048:2048 + 2 * F].rearrange("p (b f) -> p b f", b=2)
        yb = free2[:, 3072:3072 + 8 * C].bitcast(F32).rearrange("p (b c) -> p b c", b=4)
        xs_free = xs[:, :, :].rearrange("p j c -> p (j c)")
        wset = [free2[:, 4096:4096 + WSET]] + [xs_free[:, i * WSET:(i + 1) * WSET] for i in range(3)]

        names = """consts rw_in wsmall_in biases_in w1_in w2_in filled
            stats sd_ready xn_ready hi_ready lo_ready xT_tr xT_ready
            rw_ready rblk_ready folded bpq_ready biases_split w_hi w_lo
            logits counts took_ready exp_in exp_out slots_known experts_known dve
            q_proj k_proj q_expo k_expo v_proj kv_sum nums o_trans wo_out
            q_sq k_sq q_feat k_feat v_ready kv_ready o_ready oT_ready acc_ready
            rows_landed slots_tr slots_ready set_ready banks_set seeded h_ready hh_ready hl_ready y_ready y_out y_free y2_gated
            gates summed stored""".split()
        S = {n: sem(n) for n in names}
        x_in = [sem(f"x_in{i}") for i in range(4)]
        place_in = [sem(f"place_in{i}") for i in range(4)]
        scatter_in = [sem(f"scatter_in{i}") for i in range(4)]
        pieces = [(0, 2), (2, 8)] + [(t, t + 8) for t in range(8, NT, 8)]
        rows_in = [sem(f"rows_in{i}") for i in range(len(pieces))]
        y_in = [sem(f"y_in{i}") for i in range(NG)]

        block = ctx.enter_context(nc.Block())
        NW, NB = 7, 7
        XQ = NJ // 4

        at = {}

        @block.gpsimd
        def _(po):
            n = [0]

            def made(name, ins):
                ins.then_inc(S["consts"], 1)
                n[0] += 1
                at[name] = n[0]
                po.wait_ge(S["consts"], n[0])

            def select(name, t, op, basev, pattern, cm, fill_value):
                made(name, po.affine_select(out=t, in_=t, compare_op=op, fill=fill_value, base=basev, pattern=pattern,
                                            channel_multiplier=cm))

            imp = dict(allow_small_or_imprecise_dtypes=True)
            made("id16", po.memset(id16[:, :], 0.0))
            select("id16", id16[:, :], ALU.not_equal, 0, [[-1, P]], 1, 1.0)
            made("fill", po.memset(fill, 0.0))
            made("fill", po.iota(fill[:, :, 2 * C:2 * C + 2].bitcast(I32), [[P, 4]], base=PAIRS, channel_multiplier=1))
            made("xs", po.memset(xs[:, :, 2 * C:], 0.0))
            made("xs", po.iota(xs[:, :, 2 * C:2 * C + 2].bitcast(I32), [[P, NJ]], base=0, channel_multiplier=1))
            made("blk", po.memset(blk[:, :, :], 1.0))
            select("blk", blk[:, :, :], ALU.is_ge, 0, [[-HD, HEADS], [0, HD]], 1, 0.0)
            select("blk", blk[:, :, :], ALU.is_ge, HD - 1, [[HD, HEADS], [0, HD]], -1, 0.0)

            def low_parts(first, end):
                for g in range(first, end):
                    po.wait_ge(S["hi_ready"], g + 1)
                    tiles = slice(g * GT, (g + 1) * GT)
                    po.tensor_tensor(xs[:, tiles, C:2 * C], xn[:, g % (NG // 2), :, :], xs[:, tiles, 0:C],
                                     ALU.subtract).then_inc(S["lo_ready"], 1)

            po.wait_ge(S["wsmall_in"], 16 * NW)
            po.wait_ge(S["biases_in"], 16 * NB)
            made("blk", po.tensor_scalar(r_rep[:, :], r_rep[:, :], WS / HD ** 0.5, None, ALU.mult))
            po.tensor_copy(bk_wide[:, :], bqk[:, 1:2].to_broadcast([P, C])).then_inc(S["rblk_ready"], 1)
            po.tensor_tensor(rblk[:, :].rearrange("p (h d) -> p h d", d=HD), r_rep[:, :].unsqueeze(1).to_broadcast([P, HEADS, HD]),
                             blk[:, :, :], ALU.mult).then_inc(S["rblk_ready"], 1)
            low_parts(0, NG // 2)
            made("rank8", po.iota(rank8[:, :], [[-1, E]], base=E, channel_multiplier=0, **imp))
            made("onesb", po.memset(onesb[:, :], 1.0))
            made("before", po.memset(before[:, :], 1.0))
            select("before", before[:, :], ALU.is_ge, -1, [[1, P]], -1, 0.0)
            made("ones_row", po.memset(ones_row[:, :], 1.0))
            made("kb_rows", po.memset(kb_rows[:, :], 0.0))
            made("ones16", po.memset(ones16[:, :], 1.0))
            low_parts(NG // 2, NG)
            made("headof", po.memset(kvm[:, :, C:], 1.0))
            select("headof", kvm[:, :, C:], ALU.is_ge, 0, [[0, 2], [-HD, HEADS]], 1, 0.0)
            select("headof", kvm[:, :, C:], ALU.is_ge, HD - 1, [[0, 2], [HD, HEADS]], -1, 0.0)
            made("id32", po.memset(id32[:, :], 0.0))
            select("id32", id32[:, :], ALU.not_equal, 0, [[-1, P]], 1, 1.0)
            made("iota_t", po.iota(iota_t[:, :], [[1, NT + 4]], base=-1, channel_multiplier=0, **imp))
            made("b_rows", po.memset(b2_rows, 0.0))
            made("t_const", po.iota(t_const[:, :], [[0, NJ]], base=T, channel_multiplier=0))
            po.wait_ge(S["filled"], 64)
            po.wait_ge(S["slots_known"], 1)
            for i in range(2 * NJ):
                k, j = i // NJ, i % NJ
                if i >= 4:
                    po.wait_ge(place_in[i % 4], i // 4 * 16)
                if i == NJ:
                    po.wait_ge(S["slots_known"], 2)
                if k and j % 8 == 0:
                    ids = xs[:, j:j + 8, 2 * C:2 * C + 2].bitcast(I32).rearrange("p j a -> p (j a)")
                    if j == 24:
                        for u in range(4):
                            po.wait_ge(place_in[u], 16 * (NJ // 4))
                    made("second", po.tensor_tensor(ids, ids, t_const[:, 0:8], ALU.add))
                po.indirect_dma_start(out=slot_dram, out_offset=bass.IndirectOffsetOnAxis(ap=slot_i[:, i:i + 1], axis=0),
                                      in_=xs[:, j, :], in_offset=None).then_inc(place_in[i % 4], 16)
            for t in range(NT):
                if t >= 4:
                    po.wait_ge(scatter_in[t % 4], t // 4 * 16)
                    po.sem_inc(S["y_free"], 1)
                po.wait_ge(S["y_out"], t + 1)
                po.indirect_dma_start(out=y_dram, out_offset=bass.IndirectOffsetOnAxis(ap=xg[:, t, 2 * C:2 * C + 2].bitcast(I32), axis=0),
                                      in_=yb[:, t % 4, :], in_offset=None).then_inc(scatter_in[t % 4], 16)

        @block.sync
        def _(sp):
            for i in range(4):
                sp.dma_start(xin[:, i * XQ:(i + 1) * XQ, :],
                             x_rows[i * XQ * P:(i + 1) * XQ * P].rearrange("(j p) c -> p j c", p=P)).then_inc(x_in[i], 16)
            for dst, src in ((bqk[:, 0:1], bq), (bqk[:, 1:2], bk), (bv_bc[:, :], bv.partition_broadcast(P)),
                             (bo_bc[:, :], bo.partition_broadcast(P)), (b1_raw, b1),
                             (b2_raw[0:1, :, :], b2), (b2_raw[32:33, :, :], b2)):
                sp.dma_start(dst, src).then_inc(S["biases_in"], 16)
            sp.dma_start(wraw[:, :], w1T).then_inc(S["w1_in"], 16)
            sp.dma_start(wraw2[:, :], w2T).then_inc(S["w2_in"], 16)
            sp.wait_ge(S["consts"], at["fill"])
            slots_v = slot_dram.rearrange("(r u p) c -> u p r c", u=4, p=P)
            for u in range(4):
                sp.dma_start(slots_v[u], fill[:, u, :].unsqueeze(1).to_broadcast([P, NT // 4, RW])).then_inc(S["filled"], 16)
            for u in range(4):
                sp.wait_ge(place_in[u], 16 * (2 * NJ // 4))
            sp.wait_ge(S["biases_split"], 1)
            for i, (t0, t1) in enumerate(pieces):
                sp.dma_start(xg[:, t0:t1, :],
                             slot_dram[t0 * P:t1 * P].rearrange("(t p) c -> p t c", p=P)).then_inc(rows_in[i], 16)
            for i, (t0, t1) in enumerate(pieces):
                sp.wait_ge(rows_in[i], 16)
                sp.sem_inc(S["rows_landed"], t1 - t0)
            for i in range(4):
                sp.wait_ge(scatter_in[i], 16 * (NT // 4))
            sp.wait_ge(S["w_lo"], 2 * NG)
            for g in range(NG):
                for k, dst in ((0, wraw), (1, wraw2)):
                    rows = y_dram[k * T + g * GN:k * T + (g + 1) * GN]
                    sp.dma_start(dst[:, g * GN:(g + 1) * GN].rearrange("p (j c) -> p j c", c=C),
                                 rows.rearrange("(j p) c -> p j c", p=P)).then_inc(y_in[g], 16)
            for g in range(NG):
                sp.wait_ge(S["summed"], g + 1)
                sp.dma_start(out_rows[g * GN:(g + 1) * GN].rearrange("(j p) c -> p j c", p=P),
                             xin[:, g * GT:(g + 1) * GT, :]).then_inc(S["stored"], 16)
            sp.wait_ge(S["stored"], 16 * NG)

        @block.scalar
        def _(ac):
            ac.dma_start(rw_raw[:, :], rwT).then_inc(S["rw_in"], 16)
            for dst, src in ((r_rep[:, :], R), (wnat[:, 0, :], wq), (wnat[:, 1, :], wk), (w3[:, 0, :], wqT),
                             (w3[:, 1, :], wkT), (w3[:, 2, :], wvT), (wo_sb[:, :], woT)):
                ac.dma_start(dst, src).then_inc(S["wsmall_in"], 16)

            def deviation(h):
                ac.wait_ge(S["stats"], h + 1)
                ac.activation(sd[:, :], veps[:, :], ACT.Sqrt).then_inc(S["sd_ready"], 1)

            def high(g):
                ac.wait_ge(S["xn_ready"], g + 1)
                b = g % (NG // 2)
                ac.activation(xs[:, ds(g * GT, GT), 0:C], xn[:, ds(b, 1), :, :].rearrange("p a j c -> p (a j) c"),
                              ACT.Copy).then_inc(S["hi_ready"], 1)

            def transposed(g, b):
                ac.wait_ge(S["xT_tr"], g + 1)
                ac.activation(xT[:, :, ds(g * GN, GN)],
                              bank[b][:, :].bitcast(F16).rearrange("p (s n) -> p s n", s=2), ACT.Copy).then_inc(S["xT_ready"], 1)

            for g in range(NG):
                if g % (NG // 2) == 0:
                    deviation(g // (NG // 2))
                high(g)
                if g >= 2:
                    transposed(g - 2, g % 2)
            transposed(NG - 2, 0)
            transposed(NG - 1, 1)

            def weights_high(g):
                for i, raw in ((0, wraw), (2, wraw2)):
                    ac.activation(wsets[:, g * WSET + i * F:g * WSET + (i + 1) * F], raw[:, g * F:(g + 1) * F], ACT.Copy,
                                  scale=WS).then_inc(S["w_hi"], 1)

            def square(ready, g, dst, b, done):
                ac.wait_ge(ready, g + 1)
                ac.activation(dst, bank[0][:, :], ACT.Square, scale=1.0 / WS, bias=bqk[:, b:b + 1]).then_inc(done, 1)

            def features(g):
                ac.wait_ge(S["q_expo"], g + 1)
                ac.activation(qf[:, :], bank[1][:, :], ACT.Exp, scale=1.0 / WS, bias=bpq[:, 0:1]).then_inc(S["q_feat"], 1)
                ac.wait_ge(S["k_expo"], g + 1)
                ac.activation(kf[:, :, :].rearrange("p j c -> p (j c)"), bank[2][:, :], ACT.Exp, scale=1.0 / WS).then_inc(S["k_feat"], 1)

            def attended(g):
                ac.wait_ge(S["o_trans"], g + 1)
                ac.activation(oT[:, :], bank[7][:, :], ACT.Copy).then_inc(S["oT_ready"], 1)

            square(S["q_proj"], 0, q2[:, :], 0, S["q_sq"])
            square(S["k_proj"], 0, k2[:, :], 1, S["k_sq"])
            ac.wait_ge(S["bpq_ready"], 1)
            ac.wait_ge(S["w1_in"], 16)
            ac.wait_ge(S["w2_in"], 16)
            for g in range(NG):
                features(g)
                if g < NG - 1:
                    square(S["q_proj"], g + 1, q2[:, :], 0, S["q_sq"])
                if g >= 1:
                    attended(g - 1)
                if g < NG - 1:
                    square(S["k_proj"], g + 1, k2[:, :], 1, S["k_sq"])
                weights_high(g)
            ac.wait_ge(S["exp_in"], 2)
            ac.activation(ex[:, :, :], dlt[:, :, :], ACT.Exp, scale=1.0 / RS).then_inc(S["exp_out"], 1)
            ac.activation(ex2[:, :], d2[:, :], ACT.Exp, scale=1.0 / RS).then_inc(S["exp_out"], 1)

            def rows(t, b):
                ac.wait_ge(S["slots_tr"], t + 1)
                ac.activation(xgT[:, b, :, :].rearrange("p s c -> p (s c)"), bank[b][:, 0:P].bitcast(F16),
                              ACT.Copy).then_inc(S["slots_ready"], 1)

            def seed(t, u, first=False):
                ac.wait_ge(S["set_ready"], t + 1)
                if first:
                    ac.wait_ge(S["banks_set"], 1 if u < 2 else 2)
                ac.activation(hidden_bank[u][:, :].rearrange("p (f n) -> p f n", f=FC),
                              wset[u][:, WSET - 2 * FC:].bitcast(F32).unsqueeze(2).to_broadcast([P, FC, P]),
                              ACT.Copy).then_inc(S["seeded"], 1)

            def hidden(t, u):
                ac.wait_ge(S["h_ready"], t + 1)
                ac.activation(hh[:, u % 2, :], hidden_bank[u][:, :], ACT.Relu).then_inc(S["hh_ready"], 1)

            def output(t, u, wait_free=True):
                ac.wait_ge(S["y_ready"], t + 1)
                if wait_free:
                    ac.wait_ge(S["y_free"], t - 3)
                ac.activation(yb[:, u, :], bank[4 + u % 2][:, 0:C], ACT.Copy, scale=1.0 / (WS * WS)).then_inc(S["y_out"], 1)

            attended(NG - 1)
            seed(0, 0, first=True)
            rows(0, 0)
            rows(1, 1)
            seed(1, 1, first=True)
            hidden(0, 0)
            for t in range(4):
                seed(t + 2, (t + 2) % 4, first=(t < 2))
                rows(t + 2, t % 2)
                hidden(t + 1, (t + 1) % 4)
                output(t, t, wait_free=False)
            with ac.Fori(1, NT // 4 - 1) as r:
                for u in range(4):
                    seed(r * 4 + u + 2, (u + 2) % 4)
                    rows(r * 4 + u + 2, u % 2)
                    hidden(r * 4 + u + 1, (u + 1) % 4)
                    output(r * 4 + u, u)
            for t in range(NT - 4, NT):
                if t + 2 < NT:
                    seed(t + 2, (t + 2) % 4)
                    rows(t + 2, t % 2)
                if t + 1 < NT:
                    hidden(t + 1, (t + 1) % 4)
                output(t, t % 4)
            ac.wait_ge(S["gates"], 1)
            for g in range(NG):
                ac.wait_ge(y_in[g], 32)
                for j in range(g * GT, (g + 1) * GT):
                    last = ac.activation(wraw2[:, j * C:(j + 1) * C], wraw2[:, j * C:(j + 1) * C], ACT.Copy, scale=gate2[:, j:j + 1])
                last.then_inc(S["y2_gated"], 1)

        @block.vector
        def _(ve):
            n = [0]

            def step(ins):
                ins.then_inc(S["dve"], 1)
                n[0] += 1
                ve.wait_ge(S["dve"], n[0])

            ve.wait_ge(S["rw_in"], 16)
            step(ve.tensor_scalar(rw[:, 0, :], rw_raw[:, :], RS, None, ALU.mult))
            ve.scalar_tensor_tensor(rw[:, 1, :], rw_raw[:, :], RS, rw[:, 0, :], ALU.mult, ALU.subtract).then_inc(S["rw_ready"], 1)
            for h in range(2):
                for i in range(HJ):
                    j = h * HJ + i
                    if j % XQ == 0:
                        ve.wait_ge(x_in[j // XQ], 16)
                    ve.bn_stats(st6[:, i, :], xin[:, j, :])
                ve.drain()
                for i in range(HJ):
                    ve.bn_aggr(mv[:, i, :], st6[:, i, :])
                ve.drain()
                step(ve.tensor_scalar(veps[:, :], mv[:, :, 1], 1e-5, None, ALU.add))
                ve.sem_inc(S["stats"], 1)
                ve.wait_ge(S["sd_ready"], h + 1)
                step(ve.reciprocal(rs0[:, :], sd[:, :]))
                step(ve.tensor_tensor(rs1[:, :], rs0[:, :], rs0[:, :], ALU.mult))
                step(ve.tensor_tensor(rs2[:, :], rs1[:, :], veps[:, :], ALU.mult))
                step(ve.tensor_scalar(rs1[:, :], rs2[:, :], -0.5, 1.5, ALU.mult, ALU.add))
                step(ve.tensor_tensor(rstd[:, :], rs0[:, :], rs1[:, :], ALU.mult))
                for i in range(HJ):
                    if h and i % GT == 0:
                        ve.wait_ge(S["lo_ready"], i // GT + 1)
                    last = ve.tensor_scalar(xn[:, i // GT, i % GT, :], xin[:, h * HJ + i, :], mv[:, i, 0:1], rstd[:, i:i + 1],
                                            ALU.subtract, ALU.mult)
                    if i % GT == GT - 1:
                        last.then_inc(S["xn_ready"], 1)

            ve.wait_ge(S["consts"], at["kb_rows"])
            ve.wait_ge(S["wsmall_in"], 16 * NW)
            ve.wait_ge(S["biases_in"], 16 * NB)
            ve.tensor_scalar(negblk[:, :], blk[:, :, :].rearrange("p h d -> p (h d)"), -1.0, None, ALU.mult)
            ve.tensor_scalar(bv_bc[:, :], bv_bc[:, :], WS, None, ALU.mult)
            step(ve.tensor_scalar(WH[:, 0:3, :], w3[:, :, :], WS, None, ALU.mult))
            step(ve.scalar_tensor_tensor(WL[:, 0:3, :], w3[:, :, :], WS, WH[:, 0:3, :], ALU.mult, ALU.subtract))

            ve.wait_ge(S["folded"], 1)
            step(ve.tensor_copy(WH[:, 3:5, :].rearrange("p a c -> p (a c)"), bank[3][:, 0:2 * C]))
            step(ve.tensor_tensor(WL[:, 3:5, :].rearrange("p a c -> p (a c)"), bank[3][:, 0:2 * C],
                                  WH[:, 3:5, :].rearrange("p a c -> p (a c)"), ALU.subtract))
            step(ve.tensor_copy(kb_hi[:, :], bank[4][:, 0:C]))
            ve.tensor_copy(kb_rows[0:1, :], kb_hi[0:1, :])
            ve.tensor_tensor(kb_rows[32:33, :], bank[4][32:33, 0:C], kb_hi[32:33, :], ALU.subtract)
            ve.tensor_scalar(bpq[:, :], bank[4][:, C:C + 1], 1.0 / WS, None, ALU.mult).then_inc(S["bpq_ready"], 1)

            def first_max(src, m, pick, t0, t1):
                def over_e(a):
                    return a[:, t0:t1].unsqueeze(2).to_broadcast([P, t1 - t0, E])

                src, pick, eq_, sc_ = (a[:, t0:t1, :] for a in (src, pick, eq, sc))
                step(ve.tensor_reduce(m[:, t0:t1], src, AX.X, ALU.max))
                step(ve.tensor_tensor(eq_, src, over_e(m), ALU.is_equal))
                step(ve.tensor_tensor(sc_, eq_, rank8[:, :].unsqueeze(1).to_broadcast([P, t1 - t0, E]), ALU.mult))
                step(ve.tensor_reduce(mx[:, t0:t1], sc_, AX.X, ALU.max))
                step(ve.tensor_tensor(pick, sc_, over_e(mx), ALU.is_equal))

            for g0, g1 in ((0, NG - 2), (NG - 2, NG)):
                t0, t1 = g0 * GT, g1 * GT
                ve.wait_ge(S["logits"], g1)
                step(ve.tensor_copy(lg[:, t0:t1, :].rearrange("p j e -> p (j e)"), bank[6 if g0 else 7][:, t0 * E:t1 * E]))
                first_max(lg, m1, pick1, t0, t1)
                step(ve.scalar_tensor_tensor(lg2[:, t0:t1, :], pick1[:, t0:t1, :], -1e30, lg[:, t0:t1, :], ALU.mult, ALU.add))
                first_max(lg2, m2, pick2, t0, t1)
                ve.tensor_tensor(took[:, :, t0:t1].rearrange("p e j -> p j e"), pick1[:, t0:t1, :], pick2[:, t0:t1, :],
                                 ALU.add).then_inc(S["took_ready"], 1)
            def values(g):
                ve.wait_ge(S["v_proj"], g + 1)
                ve.tensor_tensor(vv[:, :, :], bank[3][:, :].rearrange("p (j c) -> p j c", j=GT),
                                 bv_bc[:, :].unsqueeze(1).to_broadcast([P, GT, C]), ALU.add).then_inc(S["v_ready"], 1)

            ve.wait_ge(S["counts"], 1)
            tot = bank[6][:, 0:E * NJ]
            ve.tensor_tensor_scan(run[:, :, :].rearrange("p e j -> p (e j)"), ones_row[:, :], tot, 0.0, ALU.mult, ALU.add)
            step(ve.tensor_reduce(cnt[:, :], tot.rearrange("p (e j) -> p e j", e=E), AX.X, ALU.add))
            ve.tensor_tensor(exc[:, :, :].rearrange("p e j -> p (e j)"), run[:, :, :].rearrange("p e j -> p (e j)"), tot, ALU.subtract)
            step(ve.tensor_scalar(cnt_i[:, :], cnt[:, :], float(P - 1), None, ALU.add))
            step(ve.tensor_scalar(nt_i[:, :], cnt_i[:, :], 7, None, ALU.arith_shift_right))
            step(ve.tensor_copy(nt_f[:, :], nt_i[:, :]))
            step(ve.tensor_tensor_scan(end_t[:, :], ones_row[:, 0:E], nt_f[:, :], 0.0, ALU.mult, ALU.add))
            step(ve.tensor_tensor(base[:, :], end_t[:, :], nt_f[:, :], ALU.subtract))
            step(ve.scalar_tensor_tensor(offs[:, :], base[:, :], float(P), exc[:, :, 0], ALU.mult, ALU.subtract))
            step(ve.tensor_tensor(pos[:, :, :].rearrange("p e j -> p (e j)"), bank[5][:, 0:E * NJ],
                                  exc[:, :, :].rearrange("p e j -> p (e j)"), ALU.add))
            step(ve.tensor_tensor(pos2[:, :, :], pos[:, :, :], offs[:, :].unsqueeze(2).to_broadcast([P, E, NJ]), ALU.add))
            for k, pick in enumerate((pick1, pick2)):
                step(ve.tensor_tensor(ppick[:, :, :], pick[:, :, :], pos2[:, :, :].rearrange("p e j -> p j e"), ALU.mult))
                step(ve.tensor_reduce(slot[:, k * NJ:(k + 1) * NJ], ppick[:, :, :], AX.X, ALU.add))
                ve.tensor_copy(slot_i[:, k * NJ:(k + 1) * NJ], slot[:, k * NJ:(k + 1) * NJ]).then_inc(S["slots_known"], 1)
                if k == 0:
                    values(0)

            def residual(g):
                ve.wait_ge(S["wo_out"], g + 1)
                ve.tensor_tensor(xin[:, ds(g * GT, GT), :], bank[7][:, :].rearrange("p (j c) -> p j c", j=GT),
                                 xin[:, ds(g * GT, GT), :], ALU.add).then_inc(S["acc_ready"], 1)

            def weights_low(g):
                ve.wait_ge(S["w_hi"], g * 2 + 2)
                for i, raw in ((0, wraw), (2, wraw2)):
                    hi, lo = (wsets[:, ds(g * WSET + (i + s) * F, F)] for s in range(2))
                    ve.scalar_tensor_tensor(lo, raw[:, ds(g * F, F)], WS, hi, ALU.mult, ALU.subtract).then_inc(S["w_lo"], 1)

            def key_values(g):
                ve.wait_ge(S["kv_sum"], g + 1)
                ve.scalar_tensor_tensor(kvm[:, :, 0:C], bank[4][:, 0:2 * C].rearrange("p (b c) -> p b c", b=2), 1.0 / WS,
                                        blk[:, :, :].rearrange("p h d -> p (h d)").unsqueeze(1).to_broadcast([P, 2, C]),
                                        ALU.mult, ALU.mult).then_inc(S["kv_ready"], 1)

            def weigh(g):
                ve.wait_ge(S["nums"], g + 1)
                for h in range(2):
                    ve.tensor_scalar(zz[:, h, :, :], bank[5 + h][:, 0:2 * NUM].rearrange("p (a c) -> p a c", a=2)[:, :, C:],
                                     1e-8, None, ALU.add)
                ve.drain()
                ve.reciprocal(zr[:, :, :, :], zz[:, :, :, :])
                ve.drain()
                for a in range(GT):
                    last = ve.tensor_tensor(oo[:, a, :].rearrange("p (h d) -> p h d", d=HD),
                                            bank[5 + a // 2][:, a % 2 * NUM:a % 2 * NUM + C].rearrange("p (h d) -> p h d", d=HD),
                                            zr[:, a // 2, a % 2, :].unsqueeze(2).to_broadcast([P, HEADS, HD]), ALU.mult)
                last.then_inc(S["o_ready"], 1)

            def plus_bo(g):
                ve.tensor_tensor(xin[:, ds(g * GT, GT), :], xin[:, ds(g * GT, GT), :],
                                 bo_bc[:, :].unsqueeze(1).to_broadcast([P, GT, C]), ALU.add)

            def dve_group(g):
                values(g)
                weigh(g - 1)
                weights_low(g - 1)
                key_values(g)
                plus_bo(g)
                residual(g - 1)

            key_values(0)
            plus_bo(0)
            dve_group(1)
            ve.wait_ge(S["consts"], at["b_rows"])
            ve.tensor_scalar(b1_cols, b1_raw, WS, None, ALU.mult)
            ve.tensor_scalar(b2_rows[0:1, :, :], b2_raw[0:1, :, :], WS * WS, None, ALU.mult)
            step(ve.tensor_scalar(b2_hi[32:33, :, :], b2_raw[32:33, :, :], WS * WS, None, ALU.mult))
            step(ve.scalar_tensor_tensor(b2_rows[32:33, :, :], b2_raw[32:33, :, :], WS * WS, b2_hi[32:33, :, :],
                                         ALU.mult, ALU.subtract))
            ve.sem_inc(S["biases_split"], 1)
            step(ve.tensor_tensor(cmp_t[:, :, :], end_t[:, :].unsqueeze(1).to_broadcast([P, NT + 4, E]),
                                  iota_t[:, :].unsqueeze(2).to_broadcast([P, NT + 4, E]), ALU.is_le))
            step(ve.tensor_reduce(et_f[:, :], cmp_t[:, :, :], AX.X, ALU.add))
            ve.tensor_scalar(et_i[:, :], et_f[:, :], float(E - 1), float(WSET), ALU.min, ALU.mult).then_inc(S["experts_known"], 1)
            ve.tensor_tensor(dlt[:, :, :], lg[:, :, :], m1[:, :].unsqueeze(2).to_broadcast([P, NJ, E]), ALU.subtract).then_inc(S["exp_in"], 1)
            ve.tensor_tensor(d2[:, :], m2[:, :], m1[:, :], ALU.subtract).then_inc(S["exp_in"], 1)
            with ve.Fori(2, NG) as g:
                dve_group(g)
            weigh(NG - 1)
            weights_low(NG - 1)
            residual(NG - 1)
            ve.wait_ge(S["exp_out"], 2)
            step(ve.tensor_reduce(ssum[:, :], ex[:, :, :], AX.X, ALU.add))
            step(ve.reciprocal(pr1[:, :], ssum[:, :]))
            step(ve.tensor_tensor(pr2[:, :], ex2[:, :], pr1[:, :], ALU.mult))
            step(ve.scalar_tensor_tensor(den[:, :], pr2[:, :], 1e-9, pr1[:, :], ALU.add, ALU.add))
            step(ve.reciprocal(rden[:, :], den[:, :]))
            ve.tensor_tensor(gate1[:, :], pr1[:, :], rden[:, :], ALU.mult)
            step(ve.tensor_tensor(gate2[:, :], pr2[:, :], rden[:, :], ALU.mult))
            ve.sem_inc(S["gates"], 1)

            regs = [ctx.enter_context(ve.register(f"set{i}")) for i in range(4)]

            def load_experts(r):
                ve.reg_load(regs, et_i[0:1, ds(r * 4, 4)])
                return [ve.snap(x, min_val=0, max_val=(E - 1) * WSET) for x in regs]

            def fetch_set(t, u, e, wait_used=True):
                if wait_used:
                    ve.wait_ge(S["y_ready"], t - 3)
                ve.tensor_copy(wset[u].bitcast(I16), wset_ints[:, ds(e, WSET)]).then_inc(S["set_ready"], 1)

            def low(t, u):
                ve.wait_ge(S["hh_ready"], t + 1)
                ve.scalar_tensor_tensor(hl[:, u % 2, :], hidden_bank[u][:, :], 0.0, hh[:, u % 2, :], ALU.max, ALU.subtract).then_inc(S["hl_ready"], 1)

            def four_tiles(r, first=False):
                e = load_experts(r + 1)
                for u in range(4):
                    t = r * 4 + u
                    fetch_set(t + 3, (u + 3) % 4, e[u], wait_used=not (first and u == 0))
                    low(t + 1, (u + 1) % 4)

            ve.wait_ge(S["experts_known"], 1)
            e = load_experts(0)
            fetch_set(0, 0, e[1], wait_used=False)
            ve.wait_ge(S["rows_landed"], 2)
            fetch_set(1, 1, e[2], wait_used=False)
            fetch_set(2, 2, e[3], wait_used=False)
            low(0, 0)
            four_tiles(0, first=True)
            with ve.Fori(1, NT // 4 - 1) as r:
                four_tiles(r)
            e = load_experts(NT // 4)
            fetch_set(NT - 1, 3, e[0])
            for u in range(1, 4):
                low(NT - 4 + u, u)

            for g in range(NG):
                ve.wait_ge(y_in[g], 32)
                for j in range(g * GT, (g + 1) * GT):
                    ve.scalar_tensor_tensor(xin[:, j, :], wraw[:, j * C:(j + 1) * C], gate1[:, j:j + 1], xin[:, j, :], ALU.mult, ALU.add)
                ve.drain()
                ve.wait_ge(S["y2_gated"], g + 1)
                tiles = slice(g * GT, (g + 1) * GT)
                ve.tensor_tensor(xin[:, tiles, :], xin[:, tiles, :], wraw2[:, g * GN:(g + 1) * GN].rearrange("p (j c) -> p j c", c=C),
                                 ALU.add).then_inc(S["summed"], 1)

        @block.tensor
        def _(pe):
            def mm(o, l, r, start=False, stop=False):
                return pe.matmul(o, l, r, start=start, stop=stop, skip_group_check=True)

            def transposes(g, b, first=False):
                pe.wait_ge(S["hi_ready"], g + 1)
                pe.wait_ge(S["lo_ready"], g + 1)
                if not first:
                    pe.wait_ge(S["xT_ready"], g - 1)
                o = bank[b][:, :].bitcast(F16)
                for s in range(2):
                    for j in range(GT):
                        to = (s * GT + j) * P
                        last = pe.transpose(o[:, to:to + P],
                                            xs[:, ds(g * GT + j, 1), s * C:(s + 1) * C].rearrange("p a c -> p (a c)"), id16[:, :])
                last.then_inc(S["xT_tr"], 1)

            def router(g):
                pe.wait_ge(S["xT_ready"], g + 1)
                for j in range(GT):
                    o = bank[7 if g < NG - 2 else 6][:, (g * GT + j) * E:(g * GT + j + 1) * E]
                    hi = xT[:, 0, ds(g * GN + j * P, P)]
                    mm(o, hi, rw[:, 0, :], start=(g in (0, NG - 2) and j == 0))
                    mm(o, hi, rw[:, 1, :])
                    last = mm(o, xT[:, 1, ds(g * GN + j * P, P)], rw[:, 0, :], stop=True)
                return last

            pe.wait_ge(S["consts"], at["id16"])
            for g in range(NG):
                transposes(g, g % 2, first=(g < 2))
                if g == 0:
                    pe.wait_ge(S["wsmall_in"], 16 * NW)
                    pe.wait_ge(S["biases_in"], 16 * NB)
                    pe.wait_ge(S["rblk_ready"], 2)
                    mm(bank[3][:, 0:C], wnat[:, 0, :], rblk[:, :], start=True, stop=True)
                    mm(bank[3][:, C:2 * C], wnat[:, 1, :], rblk[:, :], start=False, stop=True)
                    mm(bank[4][:, 0:C], bk_wide[:, :], rblk[:, :], start=True, stop=True)
                    mm(bank[4][:, C:C + 1], rblk[:, :], bqk[:, 0:1], start=False, stop=True).then_inc(S["folded"], 1)
                    pe.wait_ge(S["rw_ready"], 1)
                else:
                    router(g - 1).then_inc(S["logits"], 1)
            router(NG - 1).then_inc(S["logits"], 1)

            def count_takers():
                pe.wait_ge(S["consts"], at["before"])
                pe.wait_ge(S["took_ready"], 2)
                flat = took[:, :, :].rearrange("p e j -> p (e j)")
                mm(bank[5][:, 0:E * NJ], before[:, :], flat, start=True, stop=True)
                mm(bank[6][:, 0:E * NJ], onesb[:, :], flat, start=True, stop=True).then_inc(S["counts"], 1)

            def project(g, w):
                for n_, (a, b) in enumerate(((WH, 0), (WH, 1), (WL, 0))):
                    m = mm(bank[0][:, :], a[:, w, :], xT[:, b, ds(g * GN, GN)], start=(n_ == 0), stop=(n_ == 2))
                return m

            def project_q(g, first=False):
                if not first:
                    pe.wait_ge(S["k_sq"], g)
                project(g, Q).then_inc(S["q_proj"], 1)

            def project_k(g):
                pe.wait_ge(S["q_sq"], g + 1)
                project(g, K).then_inc(S["k_proj"], 1)

            def exponents_a(g, first=False):
                if not first:
                    pe.wait_ge(S["q_feat"], g)
                for n_, (a, b) in enumerate(((WH, 0), (WH, 1), (WL, 0))):
                    mm(bank[1][:, :], a[:, PQ, :], xT[:, b, ds(g * GN, GN)], start=(n_ == 0))
                if not first:
                    pe.wait_ge(S["k_feat"], g)
                for j in range(GT):
                    o = bank[2][:, j * P:(j + 1) * P]
                    hi, lo = (xT[:, b, ds(g * GN + j * P, P)] for b in range(2))
                    mm(o, hi, WH[:, PK, :], start=(j == 0))
                    mm(o, hi, WL[:, PK, :])
                    mm(o, lo, WH[:, PK, :])
                    mm(o, ones16[:, :], kb_rows[:, :])
                if not first:
                    pe.wait_ge(S["v_ready"], g)
                if first:
                    count_takers()
                for j in range(GT):
                    o = bank[3][:, j * P:(j + 1) * P]
                    hi, lo = (xT[:, b, ds(g * GN + j * P, P)] for b in range(2))
                    mm(o, hi, WH[:, V, :], start=(j == 0))
                    mm(o, hi, WL[:, V, :])
                    m = mm(o, lo, WH[:, V, :], stop=True)
                m.then_inc(S["v_proj"], 1)

            def exponents_b(g):
                pe.wait_ge(S["q_sq"], g + 1)
                mm(bank[1][:, :], negblk[:, :], q2[:, :], stop=True).then_inc(S["q_expo"], 1)
                pe.wait_ge(S["k_sq"], g + 1)
                for j in range(GT):
                    m = mm(bank[2][:, j * P:(j + 1) * P], k2[:, j * P:(j + 1) * P], negblk[:, :], stop=True)
                m.then_inc(S["k_expo"], 1)

            def sums(g, first=False):
                pe.wait_ge(S["k_feat"], g + 1)
                pe.wait_ge(S["v_ready"], g + 1)
                if not first:
                    pe.wait_ge(S["kv_ready"], g)
                for b in range(2):
                    for s in range(2):
                        m = mm(bank[4][:, b * C:(b + 1) * C], kf[:, 2 * b + s, :], vv[:, 2 * b + s, :],
                               start=(b == 0 and s == 0), stop=(s == 1))
                m.then_inc(S["kv_sum"], 1)

            def numerators(g, first=False):
                pe.wait_ge(S["q_feat"], g + 1)
                pe.wait_ge(S["kv_ready"], g + 1)
                if not first:
                    pe.wait_ge(S["o_ready"], g)
                for a in range(GT):
                    m = mm(bank[5 + a // 2][:, a % 2 * NUM:(a % 2 + 1) * NUM], qf[:, a * P:(a + 1) * P], kvm[:, a // 2, :],
                           start=(a % 2 == 0), stop=True)
                m.then_inc(S["nums"], 1)

            def turn(g, first=False):
                pe.wait_ge(S["o_ready"], g + 1)
                if not first:
                    pe.wait_ge(S["acc_ready"], g)
                for a in range(GT):
                    m = pe.transpose(bank[7][:, a * P:(a + 1) * P], oo[:, a, :], id32[:, :])
                m.then_inc(S["o_trans"], 1)

            def project_out(g):
                pe.wait_ge(S["oT_ready"], g + 1)
                for a in range(GT):
                    m = mm(bank[7][:, a * P:(a + 1) * P], oT[:, a * P:(a + 1) * P], wo_sb[:, :], start=(a == 0), stop=True)
                m.then_inc(S["wo_out"], 1)

            def pe_group(g, first=False, last=False):
                exponents_a(g)
                numerators(g - 1, first)
                exponents_b(g)
                if not last:
                    project_q(g + 1)
                turn(g - 1, first)
                sums(g)
                if not last:
                    project_k(g + 1)
                project_out(g - 1)

            pe.wait_ge(S["consts"], at["id32"])
            pe.wait_ge(S["bpq_ready"], 1)
            project_q(0, first=True)
            project_k(0)
            exponents_a(0, first=True)
            exponents_b(0)
            project_q(1)
            project_k(1)
            sums(0, first=True)
            pe.wait_ge(S["slots_known"], 2)
            pe_group(1, first=True)
            with pe.Fori(2, NG - 1) as g:
                pe_group(g)
            pe_group(NG - 1, last=True)

            def slots(t, b):
                pe.wait_ge(S["rows_landed"], t + 1)
                o = bank[b][:, 0:P].bitcast(F16)
                for s in range(2):
                    m = pe.transpose(o[:, s * P:(s + 1) * P], xg[:, ds(t, 1), s * C:(s + 1) * C].rearrange("p a c -> p (a c)"), id16[:, :])
                m.then_inc(S["slots_tr"], 1)

            def layer1(t, u):
                pe.wait_ge(S["slots_ready"], t + 1)
                pe.wait_ge(S["seeded"], t + 1)
                for c in range(FC):
                    o = hidden_bank[u][:, c * P:(c + 1) * P]
                    h, l = (wset[u][:, s * F + c * P:s * F + (c + 1) * P] for s in range(2))
                    mm(o, h, xgT[:, u % 2, 0, :])
                    mm(o, h, xgT[:, u % 2, 1, :])
                    m = mm(o, l, xgT[:, u % 2, 0, :], stop=(c == FC - 1))
                m.then_inc(S["h_ready"], 1)

            def layer2(t, u, first=False):
                b = u % 2
                w2h, w2l = (wset[u][:, s * F:(s + 1) * F] for s in (2, 3))
                if not first:
                    pe.wait_ge(S["y_out"], t - 1)
                o = bank[4 + b][:, 0:C]
                mm(o, ones16[:, :], wset[u][:, 4 * F:4 * F + C], start=True)
                pe.wait_ge(S["hh_ready"], t + 1)
                for c in range(FC):
                    mm(o, hh[:, b, c * P:(c + 1) * P], w2h[:, c * C:(c + 1) * C])
                    mm(o, hh[:, b, c * P:(c + 1) * P], w2l[:, c * C:(c + 1) * C])
                pe.wait_ge(S["hl_ready"], t + 1)
                for c in range(FC):
                    m = mm(o, hl[:, b, c * P:(c + 1) * P], w2h[:, c * C:(c + 1) * C], stop=(c == FC - 1))
                m.then_inc(S["y_ready"], 1)

            def four_tiles(r, first=False, last=False):
                for u in range(4):
                    t = r * 4 + u
                    if not (last and u >= 2):
                        slots(t + 2, u % 2)
                    if not (last and u == 3):
                        layer1(t + 1, (u + 1) % 4)
                    layer2(t, u, first=(first and u < 2))

            def set_banks(banks):
                for o in banks:
                    m = mm(o[:, :], id16[:, :], wsets[:, 0:F], start=True, stop=True)
                m.then_inc(S["banks_set"], 1)

            numerators(NG - 1)
            turn(NG - 1)
            set_banks(hidden_bank[:2])
            project_out(NG - 1)
            pe.wait_ge(S["acc_ready"], NG)
            set_banks(hidden_bank[2:])
            slots(0, 0)
            slots(1, 1)
            layer1(0, 0)
            four_tiles(0, first=True)
            with pe.Fori(1, NT // 4 - 1) as r:
                four_tiles(r)
            four_tiles(NT // 4 - 1, last=True)


def kernel(L0_attn_x, L0_attn_Wq, L0_attn_bq, L0_attn_Wk, L0_attn_bk, L0_attn_Wv, L0_attn_bv, L0_attn_Wo, L0_attn_bo,
           L0_attn_R, L0_ffn_router_w, L0_ffn_w1, L0_ffn_b1, L0_ffn_w2, L0_ffn_b2):
    import numpy as np
    import concourse.bacc as bacc
    from concourse.bass_utils import run_bass_kernel_spmd

    a = np.asarray
    w1, w2 = a(L0_ffn_w1), a(L0_ffn_w2)
    arrays = {
        "x": a(L0_attn_x),
        "wq": a(L0_attn_Wq), "wk": a(L0_attn_Wk),
        "wqT": a(L0_attn_Wq).T, "wkT": a(L0_attn_Wk).T, "wvT": a(L0_attn_Wv).T, "woT": a(L0_attn_Wo).T,
        "bq": a(L0_attn_bq)[:, None], "bk": a(L0_attn_bk)[:, None], "bv": a(L0_attn_bv), "bo": a(L0_attn_bo),
        "R": np.tile(a(L0_attn_R), (HEADS, 1)),
        "rwT": a(L0_ffn_router_w).T,
        "w1T": w1.transpose(2, 0, 1).reshape(C, E * F),
        "b1": a(L0_ffn_b1).reshape(E, FC, P).transpose(2, 0, 1),
        "w2T": w2.reshape(E, C, FC, P).transpose(3, 0, 2, 1).reshape(P, E * FC * C),
        "b2": a(L0_ffn_b2)[None],
    }
    arrays = {f"in_{k}": np.ascontiguousarray(v) for k, v in arrays.items()}
    nc = bacc.Bacc("TRN2", target_bir_lowering=False, num_devices=1)
    args = [nc.dram_tensor(k, v.shape, mybir.dt.from_np(v.dtype), kind="ExternalInput").ap() for k, v in arrays.items()]
    result = nc.dram_tensor("out_0", (16, 256, 128), F32, kind="ExternalOutput").ap()
    build(nc, *args, result)
    r = run_bass_kernel_spmd(nc, [arrays], core_ids=[0])
    return r.results[0]["out_0"]
```
